# Optimizing a Trainium2 kernel written in Bass

```python
import numpy as np
import jax
import jax.numpy as jnp

def _softmax(x, axis=-1):
    return jax.nn.softmax(x, axis=axis)

def _gelu(x):
    return jax.nn.gelu(x, approximate=True)

def _silu(x):
    return jax.nn.silu(x)

def _sigmoid(x):
    return jax.nn.sigmoid(x)

def _layernorm(x, axis=-1, eps=1e-05):
    m = jnp.mean(x, axis=axis, keepdims=True)
    v = jnp.var(x, axis=axis, keepdims=True)
    return (x - m) / jnp.sqrt(v + eps)

def _scatter_add(tgt, idx, src, axis=0):
    return tgt.at[idx].add(src)

def _segment_sum(src, seg, n):
    return jax.ops.segment_sum(src, seg, n)
kernel_name = 'mk_xattn_seq_d1_seqx_r8_48d724'

def setup_inputs(seed: int=0):
    np.random.seed(seed)
    _w = jnp.asarray

    def _rec_inputs():
        import jax
        import jax.numpy as jnp
        _rk = jax.random.key(seed)
        x = 7.22e-05 + 1 * jax.random.normal(jax.random.fold_in(_rk, 1), (8, 256, 128), jnp.float32)
        _lenS = 256 - jax.random.randint(jax.random.fold_in(_rk, 7), (8,), 0, max(1, 256 // 4) + 1, jnp.int32)
        _lenS2 = 1601 - jax.random.randint(jax.random.fold_in(_rk, 8), (8,), 0, max(1, 1601 // 4) + 1, jnp.int32)
        _ctx_768P = jax.random.normal(jax.random.fold_in(_rk, 11), (8, 16, 96), jnp.float32)
        _ctx_768c = jax.random.dirichlet(jax.random.fold_in(_rk, 511), 0.3 * jnp.ones((16,), jnp.float32), (8, 1601))
        _ctx_768t = jnp.einsum('bsk,bkd->bsd', _ctx_768c, _ctx_768P)
        _ctx_768t = _ctx_768t * jax.lax.rsqrt(jnp.mean(jnp.square(_ctx_768t)) + 1e-12) * 0.953939
        ctx_768 = 0.00272024 + 0.999456 * (_ctx_768t + 0.3 * jax.random.normal(jax.random.fold_in(_rk, 611), (8, 1601, 96), jnp.float32))
        return (x, ctx_768)
    x, ctx_768 = _rec_inputs()

    def _L0_xattn_setup():
        import jax, jax.numpy as jnp
        import numpy as np
        N_HEADS = 16
        D_HEAD = 64
        D_MODEL = 128
        D_COND = 96
        D_FF = 4 * D_MODEL
        EPS = 1e-05

        def _layernorm(x, g, b):
            m = jnp.mean(x, axis=-1, keepdims=True)
            v = jnp.mean(jnp.square(x - m), axis=-1, keepdims=True)
            return (x - m) * jax.lax.rsqrt(v + EPS) * g + b

        def _attention(x, cond, wq, wk, wv, wo, bo):
            B, Sq, _ = x.shape
            Sk = cond.shape[1]
            q = (x @ wq).reshape(B, Sq, N_HEADS, D_HEAD)
            k = (cond @ wk).reshape(B, Sk, N_HEADS, D_HEAD)
            v = (cond @ wv).reshape(B, Sk, N_HEADS, D_HEAD)
            scale = D_HEAD ** (-0.5)
            attn = jnp.einsum('bqhd,bkhd->bhqk', q, k) * scale
            attn = jax.nn.softmax(attn, axis=-1)
            out = jnp.einsum('bhqk,bkhd->bqhd', attn, v).reshape(B, Sq, N_HEADS * D_HEAD)
            return out @ wo + bo
        key = jax.random.key(seed)
        ks = jax.random.split(key, 16)
        d_attn = N_HEADS * D_HEAD
        s = lambda fan_in: fan_in ** (-0.5)
        inp = {'x': jax.random.normal(ks[0], (8, 128, D_MODEL), jnp.float32), 'cond': jax.random.normal(ks[1], (8, 77, D_COND), jnp.float32), 'wq1': jax.random.normal(ks[2], (D_MODEL, d_attn), jnp.float32) * s(D_MODEL), 'wk1': jax.random.normal(ks[3], (D_MODEL, d_attn), jnp.float32) * s(D_MODEL), 'wv1': jax.random.normal(ks[4], (D_MODEL, d_attn), jnp.float32) * s(D_MODEL), 'wo1': jax.random.normal(ks[5], (d_attn, D_MODEL), jnp.float32) * s(d_attn), 'bo1': jnp.zeros((D_MODEL,), jnp.float32), 'g1': jnp.ones((D_MODEL,), jnp.float32), 'b1': jnp.zeros((D_MODEL,), jnp.float32), 'wq2': jax.random.normal(ks[6], (D_MODEL, d_attn), jnp.float32) * s(D_MODEL), 'wk2': jax.random.normal(ks[7], (D_COND, d_attn), jnp.float32) * s(D_COND), 'wv2': jax.random.normal(ks[8], (D_COND, d_attn), jnp.float32) * s(D_COND), 'wo2': jax.random.normal(ks[9], (d_attn, D_MODEL), jnp.float32) * s(d_attn), 'bo2': jnp.zeros((D_MODEL,), jnp.float32), 'g2': jnp.ones((D_MODEL,), jnp.float32), 'b2': jnp.zeros((D_MODEL,), jnp.float32), 'w_ff1': jax.random.normal(ks[10], (D_MODEL, 2 * D_FF), jnp.float32) * s(D_MODEL), 'b_ff1': jnp.zeros((2 * D_FF,), jnp.float32), 'w_ff2': jax.random.normal(ks[11], (D_FF, D_MODEL), jnp.float32) * s(D_FF), 'b_ff2': jnp.zeros((D_MODEL,), jnp.float32), 'g3': jnp.ones((D_MODEL,), jnp.float32), 'b3': jnp.zeros((D_MODEL,), jnp.float32)}
        return inp
    _L0_xattn_all = _L0_xattn_setup()
    _L0_xattn_in = {k: v for k, v in _L0_xattn_all.items() if k in ('wq1', 'wk1', 'wv1', 'wo1', 'bo1', 'g1', 'b1', 'wq2', 'wk2', 'wv2', 'wo2', 'bo2', 'g2', 'b2', 'w_ff1', 'b_ff1', 'w_ff2', 'b_ff2', 'g3', 'b3')}
    del _L0_xattn_all
    return {'x': x, 'ctx_768': ctx_768, 'L0_xattn_wq1': _L0_xattn_in['wq1'], 'L0_xattn_wk1': _L0_xattn_in['wk1'], 'L0_xattn_wv1': _L0_xattn_in['wv1'], 'L0_xattn_wo1': _L0_xattn_in['wo1'], 'L0_xattn_bo1': _L0_xattn_in['bo1'], 'L0_xattn_g1': _L0_xattn_in['g1'], 'L0_xattn_b1': _L0_xattn_in['b1'], 'L0_xattn_wq2': _L0_xattn_in['wq2'], 'L0_xattn_wk2': _L0_xattn_in['wk2'], 'L0_xattn_wv2': _L0_xattn_in['wv2'], 'L0_xattn_wo2': _L0_xattn_in['wo2'], 'L0_xattn_bo2': _L0_xattn_in['bo2'], 'L0_xattn_g2': _L0_xattn_in['g2'], 'L0_xattn_b2': _L0_xattn_in['b2'], 'L0_xattn_w_ff1': _L0_xattn_in['w_ff1'], 'L0_xattn_b_ff1': _L0_xattn_in['b_ff1'], 'L0_xattn_w_ff2': _L0_xattn_in['w_ff2'], 'L0_xattn_b_ff2': _L0_xattn_in['b_ff2'], 'L0_xattn_g3': _L0_xattn_in['g3'], 'L0_xattn_b3': _L0_xattn_in['b3']}

def reference(x, ctx_768, L0_xattn_wq1, L0_xattn_wk1, L0_xattn_wv1, L0_xattn_wo1, L0_xattn_bo1, L0_xattn_g1, L0_xattn_b1, L0_xattn_wq2, L0_xattn_wk2, L0_xattn_wv2, L0_xattn_wo2, L0_xattn_bo2, L0_xattn_g2, L0_xattn_b2, L0_xattn_w_ff1, L0_xattn_b_ff1, L0_xattn_w_ff2, L0_xattn_b_ff2, L0_xattn_g3, L0_xattn_b3):
    import jax
    import jax.numpy as jnp

    def _L0_xattn_ref(x, cond, wq1, wk1, wv1, wo1, bo1, g1, b1, wq2, wk2, wv2, wo2, bo2, g2, b2, w_ff1, b_ff1, w_ff2, b_ff2, g3, b3):
        import jax, jax.numpy as jnp
        import numpy as np
        N_HEADS = 16
        D_HEAD = 64
        D_MODEL = 128
        D_COND = 96
        D_FF = 4 * D_MODEL
        EPS = 1e-05

        def _layernorm(x, g, b):
            m = jnp.mean(x, axis=-1, keepdims=True)
            v = jnp.mean(jnp.square(x - m), axis=-1, keepdims=True)
            return (x - m) * jax.lax.rsqrt(v + EPS) * g + b

        def _attention(x, cond, wq, wk, wv, wo, bo):
            B, Sq, _ = x.shape
            Sk = cond.shape[1]
            q = (x @ wq).reshape(B, Sq, N_HEADS, D_HEAD)
            k = (cond @ wk).reshape(B, Sk, N_HEADS, D_HEAD)
            v = (cond @ wv).reshape(B, Sk, N_HEADS, D_HEAD)
            scale = D_HEAD ** (-0.5)
            attn = jnp.einsum('bqhd,bkhd->bhqk', q, k) * scale
            attn = jax.nn.softmax(attn, axis=-1)
            out = jnp.einsum('bhqk,bkhd->bqhd', attn, v).reshape(B, Sq, N_HEADS * D_HEAD)
            return out @ wo + bo
        h = _layernorm(x, g1, b1)
        x = _attention(h, h, wq1, wk1, wv1, wo1, bo1) + x
        h = _layernorm(x, g2, b2)
        x = _attention(h, cond, wq2, wk2, wv2, wo2, bo2) + x
        h = _layernorm(x, g3, b3)
        proj = h @ w_ff1 + b_ff1
        a, gate = jnp.split(proj, 2, axis=-1)
        ff = a * jax.nn.gelu(gate, approximate=False) @ w_ff2 + b_ff2
        return ff + x
    x = _L0_xattn_ref(x, ctx_768, L0_xattn_wq1, L0_xattn_wk1, L0_xattn_wv1, L0_xattn_wo1, L0_xattn_bo1, L0_xattn_g1, L0_xattn_b1, L0_xattn_wq2, L0_xattn_wk2, L0_xattn_wv2, L0_xattn_wo2, L0_xattn_bo2, L0_xattn_g2, L0_xattn_b2, L0_xattn_w_ff1, L0_xattn_b_ff1, L0_xattn_w_ff2, L0_xattn_b_ff2, L0_xattn_g3, L0_xattn_b3)
    return x

_drawn_inputs = setup_inputs


def setup_inputs(seed=0):
    import zlib

    import numpy as np

    out = dict(_drawn_inputs(seed))
    spreads = {'L0_xattn_bo1': (0.0, 0.1),
     'L0_xattn_g1': (1.0, 0.2),
     'L0_xattn_b1': (0.0, 0.1),
     'L0_xattn_bo2': (0.0, 0.1),
     'L0_xattn_g2': (1.0, 0.2),
     'L0_xattn_b2': (0.0, 0.38),
     'L0_xattn_b_ff1': (0.0, 0.1),
     'L0_xattn_b_ff2': (0.0, 0.1),
     'L0_xattn_g3': (1.0, 0.2),
     'L0_xattn_b3': (0.0, 0.1)}
    factors = {}
    for name, (base, spread) in spreads.items():
        noise = np.random.default_rng([zlib.crc32(name.encode()), seed]).standard_normal(out[name].shape)
        drawn = base * np.exp(spread * noise) if base else spread * noise
        out[name] = jnp.asarray(drawn.astype(out[name].dtype))
    for name, factor in factors.items():
        out[name] = (out[name] * factor).astype(out[name].dtype)
    return out
```

```python
from contextlib import ExitStack

import concourse.bass as bass
from concourse import mybir

F32 = mybir.dt.float32
F32R = mybir.dt.float32r
ACT = mybir.ActivationFunctionType
ALU = mybir.AluOpType
AX = mybir.AxisListType

P = 128
AUG = 96
EPS = 1e-5
PAIR = 2
NPS = 3


class Shapes:
    def __init__(self, x, ctx, wq, wff1):
        self.B, self.SQ, self.D = x.shape
        _, self.SK, self.DC = ctx.shape
        self.HD = wq.shape[1]
        self.DH = 64
        self.H = self.HD // self.DH
        self.NP = self.H // PAIR
        self.QT = self.SQ // P
        self.W = PAIR * self.SQ
        self.NSLAB = self.B * self.QT
        self.HC = self.HD // P
        self.FF = wff1.shape[1] // 2
        self.FC = self.FF // P
        self.CT = -(-self.SK // P)
        self.CLAST = self.SK - (self.CT - 1) * P
        assert self.D == P and self.DC == AUG and self.W == 512 and self.SQ == 256
        assert self.NP == 8 and self.B == 8 and self.CLAST > 64 and self.CT % 2


def count(value):
    return max(value, 0) if isinstance(value, int) else value


class Stage:

    def __init__(self, name, nt, krows, drows, qrows, ahead, nq, mx_groups, mx_per_batch, ring):
        self.name = name
        self.nt = nt
        self.krows = krows
        self.drows = drows
        self.qrows = qrows
        self.ahead = ahead
        self.nq = nq
        self.mx_groups = mx_groups
        self.mx_per_batch = mx_per_batch
        self.ring = ring

    def bank(self, hp, t):
        return self.ring[(hp * self.nt + t) % len(self.ring)]

    def back(self, hp, t):
        n, i = len(self.ring), hp * self.nt + t
        return next(k for k in range(1, n + 1) if self.ring[(i - k) % n] == self.ring[i % n])


class Pair:

    def __init__(self, b, bs, hp, np_):
        self.b, self.bs, self.hp, self.np_ = b, bs, hp, np_
        self.g = b * np_ + hp

    def next(self, n, last_b):
        if self.hp + n < self.np_:
            return Pair(self.b, self.bs, self.hp + n, self.np_)
        if last_b:
            return None
        return Pair(self.b + 1, self.bs + 1, self.hp + n - self.np_, self.np_)


def build(nc, x, ctx, w, out):
    sh = Shapes(x, ctx, w["wq1"], w["w_ff1"])
    B, SQ, D, H, NP_, QT, W, CT, DC = sh.B, sh.SQ, sh.D, sh.H, sh.NP, sh.QT, sh.W, sh.CT, sh.DC
    NSLAB, HC, FC, HD = sh.NSLAB, sh.HC, sh.FC, sh.HD
    SCALE = float(sh.DH) ** -0.5
    SKP = CT * P
    MXW = [402, 400, 400, 400]
    MX0 = [0, 402, 802, 1202]
    assert MX0[-1] + MXW[-1] == sh.SK + sh.SK % 2

    SELF = Stage("self", QT, [P] * QT, P, P, 3, 4, 2, 0, [0, 1, 2, 0, 1, 2, 0, 1])
    CROSS = Stage("cross", CT, [P] * (CT - 1) + [sh.CLAST], DC + 1, DC, 2, 4, 16, 4,
                  [t % NPS for t in range(CT)] + [(t + 1) % NPS for t in range(CT)])
    STAGES = (SELF, CROSS)

    with ExitStack() as stack:
        stack.enter_context(nc.allow_non_contiguous_dma(reason="columns of at most 512 values"))

        def sb(name, shape, dt=F32):
            return stack.enter_context(nc.sbuf_tensor(name, shape, dt))

        def sem(name):
            return stack.enter_context(nc.semaphore(name))

        xs = sb("xs", [P, NSLAB, D])
        z = sb("z", [P, NSLAB, D])
        zt = sb("zt", [P, NSLAB * P])
        stats = sb("stats", [P, NSLAB, 6])
        mv = sb("mv", [P, NSLAB, 2])
        veps = sb("veps", [P, NSLAB])
        rstd = sb("rstd", [P, NSLAB])
        mhalf = sb("mhalf", [P, NSLAB])
        zeros = sb("zeros", [P, CT, 1])
        ident = sb("ident", [P, P])
        fold = sb("fold", [P, P])
        gcol = sb("gcol", [P, 3])
        bcol = sb("bcol", [P, 3])
        mt = sb("mt", [P, 4, P])
        bo = sb("bo", [P, 3, D])
        bff1 = sb("bff1", [P, 2 * FC])
        raw = sb("raw", [P, 3, HD])
        wo = sb("wo", [P, HC, D])
        wt = sb("wt", [P, 3, HC, P])
        a_hi = sb("a_hi", [P, H, P], F32R)
        a_lo = sb("a_lo", [P, H, P], F32R)
        bm = sb("bm", [P, H, D + 2])
        zt_hi = sb("zt_hi", [P, 2, SQ], F32R)
        zt_lo = sb("zt_lo", [P, 2, SQ], F32R)
        zn_hi = sb("zn_hi", [P, 2, QT, P], F32R)
        zn_lo = sb("zn_lo", [P, 2, QT, P], F32R)
        craw = sb("craw", [P, CT, DC])
        ct_hi = sb("ct_hi", [DC + 1, 2, SKP], F32R)
        ct_lo = sb("ct_lo", [DC + 1, 2, SKP], F32R)
        cn_hi = sb("cn_hi", [P, 2, CT, DC + 2], F32R)
        cn_lo = sb("cn_lo", [P, 2, CT, DC + 2], F32R)
        q_hi = sb("q_hi", [P, 4, W], F32R)
        q_lo = sb("q_lo", [P, 4, W], F32R)
        p_32 = sb("p_32", [P, NPS, W])
        p_hi = sb("p_hi", [P, NPS, W], F32R)
        p_lo = sb("p_lo", [P, NPS, W], F32R)
        mxp = sb("mxp", [P, 4, 4, 4])
        negm = sb("negm", [P, 4, 4], F32R)
        u_sb = sb("u_sb", [P, W])
        rden = sb("rden", [P, 4])
        w1_hi = sb("w1_hi", [P, 2 * sh.FF], F32R)
        w1_lo = sb("w1_lo", [P, 2 * sh.FF], F32R)
        w2 = sb("w2", [P, FC, D])

        banks = [stack.enter_context(nc.psum_tensor(f"bank{i}", [P, 512], F32)) for i in range(8)]
        s_ps = banks[0:3]
        u_ps = banks[3]
        mx_ps = banks[4:6]
        o_ps = banks[6]
        m_ps = banks[7]

        x_in, wts_in, small_in, consts, ctx_in, stored = (
            sem(n) for n in ("x_in", "wts_in", "small_in", "consts", "ctx_in", "stored"))
        wo_in, ff_in = sem("wo_in"), sem("ff_in")
        var_ready, rstd_made = sem("var_ready"), sem("rstd_made")
        mt_made, ln_step, z_made, zt_ready, zt_copied, bias_added = (
            sem(n) for n in ("mt_made", "ln_step", "z_made", "zt_ready", "zt_copied", "bias_added"))
        w_ready, w_hi, w_out, bm_set, ones_set, mt_step = (
            sem(n) for n in ("w_ready", "w_hi", "w_out", "bm_set", "ones_set", "mt_step"))
        S = {}
        for st in STAGES:
            S[st.name] = {n: sem(f"{st.name}_{n}") for n in (
                "scores_ready", "exp_done", "plo_done", "pv_done", "q_ready", "qhi_done", "qlo_done",
                "mx_ready", "mx_read", "negm_ready", "u_copied", "out_ready", "rden_made",
                "half_added", "out_read", "zhi_done", "zlo_done", "chi_done", "vhi_done",
                "vlo_done")}
        for st in STAGES:
            S[st.name]["mrow_in"] = [sem(f"{st.name}_mrow_in{k}") for k in range(st.nq)]
        ff1_ready, gelu_done, act_done, ff2_ready, ff_added = (
            sem(n) for n in ("ff1_ready", "gelu_done", "act_done", "ff2_ready", "ff_added"))
        ffz_hi, ffz_lo = sem("ffz_hi"), sem("ffz_lo")

        def pairs(eng, st, body):
            def batch(b, bs, last):
                for hp in range(NP_):
                    body(Pair(b, bs, hp, NP_), last)

            batch(0, 0, False)
            with eng.Fori(0, (B - 2) // 2) as i:
                for k in range(2):
                    batch(i * 2 + (1 + k), 1 + k, False)
            batch(B - 1, B - 1, True)

        def ahead_pairs(st):
            return [Pair(0, 0, n, NP_) for n in range(st.ahead)]

        def needs_prep(st, pr, last):
            return not last and pr.hp + st.ahead == NP_

        def mx_count(st, pr):
            return pr.g * st.mx_groups + (pr.b + 1) * st.mx_per_batch

        def plan(st, pr, last):
            steps = [[] for _ in range(st.nt)]
            nxt = pr.next(st.ahead, last)
            prep = nxt and needs_prep(st, pr, last)
            if st is SELF:
                if prep:
                    steps[0].append(("prep", range(1)))
                if nxt:
                    steps[0].append(("q", None))
                    steps[1].append(("mx", range(2)))
                steps[1].append(("out", None))
                return steps, nxt
            if prep:
                for k in range(4):
                    steps[k].append(("prep", range(k, k + 1)))
            if nxt:
                steps[0].append(("q", None))
                n0 = 4 if prep else 1
                left = CT - n0
                for k in range(left):
                    steps[n0 + k].append(("mx", range(16 * k // left, 16 * (k + 1) // left)))
            steps[2].append(("out", None))
            return steps, nxt

        CGROUPS = [range(0, 4), range(4, 8), range(8, 12), range(12, CT)]
        NWG = 14

        def width(n):
            return (len(CGROUPS[n]) - 1) * P + (sh.CLAST if n == len(CGROUPS) - 1 else P)

        def heads(t, half, odd, c):
            return t[:, 8 * half + odd:8 * half + odd + 7:2, 0:c]

        def fill_bank(fill):
            return s_ps[fill % 3]

        def fill_view(fill, c, rows=P):
            return fill_bank(fill)[0:rows, 0:4 * c].rearrange("p (h c) -> p h c", h=4)

        gate_ps = [s_ps[0], mx_ps[0]]
        lin_ps = [s_ps[1], mx_ps[1]]
        ff2_ps = [s_ps[2], u_ps]

        def ffx(c):
            t = wt[:, 0:2].rearrange("p a c d -> p (a c d)") if c % 2 == 0 else raw[:, 1:3].rearrange("p a c -> p (a c)")
            return t

        block = stack.enter_context(nc.Block())

        def load_context(sp, b):
            full = (CT - 1) * P
            one = isinstance(b, int)
            src = ctx[b] if one else ctx[bass.ds(b, 1)].rearrange("o s d -> (o s) d")
            sp.dma_start(craw[:, 0:CT - 1, :], src[0:full, :].rearrange("(t p) d -> p t d", p=P)).then_inc(ctx_in, 16)
            sp.dma_start(craw[0:sh.CLAST, CT - 1, :], src[full:sh.SK, :]).then_inc(ctx_in, 16)

        def mrows(sp, st):
            s = S[st.name]

            def row(pr):
                if st is SELF:
                    sp.wait_ge(s["mx_read"], mx_count(st, pr) + st.mx_groups)
                else:
                    sp.wait_ge(s["negm_ready"], pr.g + 1)
                q = pr.hp % st.nq
                for j in range(4):
                    sp.dma_start(q_hi[AUG:AUG + 1, q, j * P:(j + 1) * P].bitcast(F32),
                                 negm[:, q, j:j + 1].bitcast(F32)).then_inc(s["mrow_in"][q], 16)

            def body(pr, last):
                if st is CROSS and pr.hp == 0 and not last:
                    sp.wait_ge(s["vlo_done"], 2 * pr.b + 2)
                    sp.wait_ge(s["mx_ready"], (pr.b + 1) * 4 + pr.b * 128)
                    load_context(sp, pr.b + 1)
                nxt = pr.next(st.ahead, last)
                if nxt:
                    row(nxt)

            for pr in ahead_pairs(st):
                row(pr)
            pairs(sp, st, body)

        @block.sync
        def _(sp):
            sp.dma_start(xs[:], x.rearrange("b (t p) d -> p (b t) d", p=P)).then_inc(x_in, 16)
            for i in (1, 2, 3):
                sp.dma_start(gcol[:, i - 1:i], w[f"g{i}"].rearrange("(p o) -> p o", o=1)).then_inc(small_in, 16)
                sp.dma_start(bcol[:, i - 1:i], w[f"b{i}"].rearrange("(p o) -> p o", o=1)).then_inc(small_in, 16)
            for i, n in enumerate(("wq1", "wk1", "wv1")):
                sp.dma_start(raw[:, i, :], w[n]).then_inc(wts_in, 16)
            sp.dma_start(wo[:], w["wo1"].rearrange("(c p) d -> p c d", p=P)).then_inc(wo_in, 16)
            for i, n in enumerate(("bo1", "bo2", "b_ff2")):
                sp.dma_start(bo[:, i, :], w[n].rearrange("(o d) -> o d", o=1).to_broadcast([P, D])).then_inc(small_in, 16)
            sp.dma_start(bff1[:], w["b_ff1"].rearrange("(c p) -> p c", p=P)).then_inc(small_in, 16)
            load_context(sp, 0)
            mrows(sp, SELF)
            sp.wait_ge(w_out, NWG)
            for i, n in enumerate(("wq2", "wk2", "wv2")):
                sp.dma_start(raw[0:w[n].shape[0], i, :], w[n]).then_inc(wts_in, 16)
            sp.dma_start(wo[:], w["wo2"].rearrange("(c p) d -> p c d", p=P)).then_inc(wo_in, 16)
            sp.wait_ge(w_out, 2 * NWG)
            sp.dma_start(raw[:, 0, :], w["w_ff1"]).then_inc(ff_in, 16)
            sp.dma_start(w2[:], w["w_ff2"].rearrange("(c p) d -> p c d", p=P)).then_inc(ff_in, 16)
            mrows(sp, CROSS)
            for c in range(4):
                sp.wait_ge(ff_added, c + 1)
                sp.dma_start(out.rearrange("b (t p) d -> p (b t) d", p=P)[:, 4 * c:4 * c + 4, :],
                             xs[:, 4 * c:4 * c + 4, :]).then_inc(stored, 16)
            sp.wait_ge(stored, 4 * 16)

        def split_context(pool, b, kp):
            s = S["cross"]
            pool.wait_ge(ctx_in, (b + 1) * 32)
            for n, (hi, t0, t1) in enumerate(((P, 0, CT - 1), (sh.CLAST, CT - 1, CT))):
                pool.wait_ge(s["vlo_done"], 2 * b + n)
                nc.gpsimd.tensor_tensor(out=cn_hi[0:hi, kp, t0:t1, 0:DC], in0=craw[0:hi, t0:t1, :],
                                        in1=zeros[0:hi, 0:t1 - t0, 0:1].to_broadcast([hi, t1 - t0, DC]),
                                        op=ALU.add).then_inc(s["vhi_done"], 1)
                pool.wait_ge(s["vhi_done"], 2 * b + n + 1)
                nc.gpsimd.tensor_tensor(out=cn_lo[0:hi, kp, t0:t1, 0:DC], in0=craw[0:hi, t0:t1, :],
                                        in1=cn_hi[0:hi, kp, t0:t1, 0:DC].bitcast(F32),
                                        op=ALU.subtract).then_inc(s["vlo_done"], 1)

        @block.gpsimd
        def _(pool):
            g = nc.gpsimd
            g.memset(ident[:], 0.0).then_inc(consts, 1)
            pool.wait_ge(consts, 1)
            g.affine_select(out=ident[:], in_=ident[:], compare_op=ALU.not_equal, fill=1.0, base=0,
                            pattern=[[-1, P]], channel_multiplier=1).then_inc(consts, 1)
            pool.wait_ge(consts, 2)
            g.affine_select(out=fold[:], in_=ident[:], compare_op=ALU.not_equal, fill=-1.0, base=-AUG,
                            pattern=[[0, P]], channel_multiplier=1).then_inc(consts, 1)
            g.memset(mhalf[:], -0.5).then_inc(consts, 1)
            g.memset(zeros[:], 0.0).then_inc(consts, 1)
            g.memset(bm[:], 0.0).then_inc(bm_set, 1)
            pool.wait_ge(bm_set, 1)
            g.memset(bm[AUG:AUG + 1, :, D:D + 1], 1.0).then_inc(bm_set, 1)
            g.memset(ct_hi[AUG:AUG + 1].bitcast(F32), 1.0).then_inc(ones_set, 1)
            pool.wait_ge(ones_set, 1)
            g.memset(cn_hi[:, :, :, DC:DC + 2].bitcast(F32), 1.0).then_inc(ones_set, 1)
            g.memset(cn_lo[:, :, :, DC:DC + 2].bitcast(F32), 0.0).then_inc(ones_set, 1)
            pool.wait_ge(small_in, 10 * 16)
            for n in range(3):
                if n == 1:
                    pool.wait_ge(S["self"]["out_ready"], B * NP_)
                    g.memset(bm[AUG:AUG + 1, :, 0:D], 0.0).then_inc(bm_set, 1)
                    pool.wait_ge(bm_set, 3)
                for c in range(4):
                    cols = slice(4 * c, 4 * c + 4)
                    if c == 0:
                        pool.wait_ge(consts, 5)
                    pool.wait_ge(var_ready, 4 * n + c + 1)
                    g.tensor_tensor(out=rstd[:, cols], in0=veps[:, cols], in1=mhalf[:, cols],
                                    op=ALU.pow).then_inc(rstd_made, 1)
                    pool.wait_ge(z_made, 4 * n + c + 1)
                    v = xs[:, 4 * c:4 * c + 4, :]
                    g.tensor_tensor(out=v, in0=v, in1=bo[:, n:n + 1, :].to_broadcast([P, 4, D]),
                                    op=ALU.add).then_inc(bias_added, 1)
                if n == 1:
                    s = S["cross"]
                    split_context(pool, 0, 0)

                    def body(pr, last):
                        if needs_prep(CROSS, pr, last):
                            if not (isinstance(pr.b, int) and pr.b == 0):
                                pool.wait_ge(s["pv_done"], pr.b * (NP_ * CT))
                            split_context(pool, pr.b + 1, (pr.bs + 1) % 2)

                    pairs(pool, CROSS, body)

        @block.scalar
        def _(act):
            def copy(dst, src):
                return nc.scalar.activation(dst, src, ACT.Copy)

            def weights(n):
                for k in range(4):
                    fill = NWG * n + 6 + k
                    act.wait_ge(w_ready, fill + 1)
                    odd, half = k // 2, k % 2
                    c = P if n == 0 else DC
                    copy(heads(a_hi, half, odd, c), fill_view(fill, c)).then_inc(w_hi, 1)

            def layer_norm(n):
                for c in range(4):
                    act.wait_ge(zt_ready, 4 * n + c + 1)
                    copy(zt[:, c * 512:(c + 1) * 512], o_ps[:] if c % 2 == 0 else m_ps[:]).then_inc(zt_copied, 1)

            def attention(st):
                s = S[st.name]

                def z_parts(b, kp):
                    off = b * SQ
                    i = copy(zt_hi[:, kp, :], zt[:, bass.ds(off, SQ)])
                    if st is SELF:
                        i = copy(zn_hi[:, kp, :, :], z[:, bass.ds(b * QT, QT), :])
                    i.then_inc(s["zhi_done"], 1)

                def prep(b, kp, groups):
                    if st is SELF:
                        z_parts(b, kp)
                        return
                    for n in groups:
                        if n == 0:
                            z_parts(b, kp)
                        fill = b * (16 * NP_ + 4) + n
                        act.wait_ge(s["mx_ready"], fill + 1)
                        cols = slice(CGROUPS[n][0] * P, CGROUPS[n][0] * P + width(n))
                        copy(ct_hi[0:DC, kp, cols], mx_ps[n % 2][0:DC, 0:width(n)]).then_inc(s["chi_done"], 1)

                def queries(pr):
                    act.wait_ge(s["q_ready"], pr.g + 1)
                    copy(q_hi[0:st.qrows, pr.hp % st.nq, :], m_ps[0:st.qrows, :]).then_inc(s["qhi_done"], 1)

                def u_copy(g):
                    act.wait_ge(s["pv_done"], (g + 1) * st.nt)
                    act.wait_ge(s["out_ready"], count(g))
                    copy(u_sb[0:st.drows, :], u_ps[0:st.drows, :]).then_inc(s["u_copied"], 1)

                def body(pr, last):
                    steps, nxt = plan(st, pr, last)
                    for t in range(st.nt):
                        r, k = pr.g * st.nt + t, st.bank(pr.hp, t)
                        kr = st.krows[t]
                        act.wait_ge(s["scores_ready"], r + 1)
                        act.wait_ge(s["pv_done"], count(r - st.back(pr.hp, t) + 1))
                        nc.scalar.activation(p_32[0:kr, k, :], s_ps[k][0:kr, :], ACT.Exp, scale=SCALE)
                        nc.scalar.activation(p_hi[0:kr, k, :], s_ps[k][0:kr, :], ACT.Exp,
                                             scale=SCALE).then_inc(s["exp_done"], 1)
                        if t == 0 and not (isinstance(pr.g, int) and pr.g == 0):
                            u_copy(pr.g - 1)
                        for what, arg in steps[t]:
                            if what == "prep":
                                prep(pr.b + 1, (pr.bs + 1) % 2, arg)
                            if what == "q":
                                queries(nxt)

                prep(0, 0, range(4))
                for pr in ahead_pairs(st):
                    queries(pr)
                pairs(act, st, body)
                u_copy(B * NP_ - 1)

            weights(0)
            layer_norm(0)
            act.wait_ge(zt_copied, 4)
            attention(SELF)
            weights(1)
            layer_norm(1)
            act.wait_ge(zt_copied, 8)
            attention(CROSS)
            for k in range(2):
                act.wait_ge(w_ready, 2 * NWG + k + 1)
                copy(w1_hi[:, k * 512:(k + 1) * 512], s_ps[(2 * NWG + k) % 3][:]).then_inc(w_hi, 1)
            layer_norm(2)
            for c in range(4):
                act.wait_ge(zt_copied, 8 + c + 1)
                act.wait_ge(ff1_ready, count(8 * (c - 1)))
                copy(q_hi[:, c % 2, :], zt[:, c * 512:(c + 1) * 512]).then_inc(ffz_hi, 1)
                for f in range(FC):
                    act.wait_ge(ff1_ready, 8 * c + 2 * f + 1)
                    act.wait_ge(act_done, count(FC * c + f - 1))
                    nc.scalar.activation(p_32[:, f % 2, :], gate_ps[f % 2][:], ACT.Gelu,
                                         bias=bff1[:, FC + f:FC + f + 1]).then_inc(gelu_done, 1)

        @block.vector
        def _(dve):
            v = nc.vector

            def weights(n):
                rows = P if n == 0 else DC
                for m in range(3):
                    c = P if m == 0 else rows
                    for k in range(2):
                        fill = NWG * n + 2 * m + k
                        dve.wait_ge(w_ready, fill + 1)
                        v.tensor_copy(wt[:, m, 4 * k:4 * k + 4, 0:c], fill_view(fill, c)).then_inc(w_out, 1)
                for k in range(4):
                    fill = NWG * n + 6 + k
                    odd, half = k // 2, k % 2
                    dve.wait_ge(w_hi, 4 * n + k + 1)
                    v.tensor_tensor(out=heads(a_lo, half, odd, rows), in0=fill_view(fill, rows),
                                    in1=heads(a_hi, half, odd, rows).bitcast(F32), op=ALU.subtract).then_inc(w_out, 1)
                dve.wait_ge(bm_set, 2 + n)
                for k in range(4):
                    fill = NWG * n + 10 + k
                    odd, half = k // 2, k % 2
                    dve.wait_ge(w_ready, fill + 1)
                    v.tensor_copy(heads(bm, half, odd, D)[0:rows], fill_view(fill, D, rows)).then_inc(w_out, 1)

            def make_mt():
                dve.wait_ge(small_in, 160)
                dve.wait_ge(consts, 3)
                for k, i in enumerate((0, 0, 1, 2)):
                    v.tensor_scalar(mt[:, k, :], fold[:], gcol[:, i:i + 1], None, ALU.mult).then_inc(mt_step, 1)
                dve.wait_ge(mt_step, 4)
                for k, i in enumerate((0, None, 1, 2)):
                    col = mt[:, k, AUG:AUG + 1]
                    if i is None:
                        ins = v.memset(col, 0.0)
                    else:
                        ins = v.tensor_copy(col, bcol[:, i:i + 1])
                    ins.then_inc(mt_made, 1)

            def layer_norm(n):
                step = [ln_count[0]]

                def done(ins):
                    step[0] += 1
                    ins.then_inc(ln_step, 1)

                for c in range(4):
                    slabs = range(4 * c, 4 * c + 4)
                    if n:
                        dve.wait_ge(zt_ready, 4 * n)
                    for i in slabs:
                        done(v.bn_stats(stats[:, i, :], xs[:, i, :]))
                    dve.wait_ge(ln_step, step[0])
                    for i in slabs:
                        done(v.bn_aggr(mv[:, i, :], stats[:, i, :]))
                    dve.wait_ge(ln_step, step[0])
                    v.tensor_scalar(veps[:, 4 * c:4 * c + 4], mv[:, 4 * c:4 * c + 4, 1], EPS, None, ALU.add).then_inc(var_ready, 1)
                    dve.wait_ge(rstd_made, 4 * n + c + 1)
                    for i in slabs:
                        done(v.tensor_scalar(z[:, i, :], xs[:, i, :], mv[:, i, 0:1], rstd[:, i:i + 1],
                                             ALU.subtract, ALU.mult))
                    dve.wait_ge(ln_step, step[0])
                    v.memset(z[:, 4 * c:4 * c + 4, AUG:AUG + 1], 1.0).then_inc(z_made, 1)
                ln_count[0] = step[0]

            ln_count = [0]

            def attention(st):
                s = S[st.name]

                def z_parts(b, kp):
                    dve.wait_ge(s["zhi_done"], b + 1)
                    i = v.tensor_tensor(out=zt_lo[:, kp, :], in0=zt[:, bass.ds(b * SQ, SQ)],
                                        in1=zt_hi[:, kp, :].bitcast(F32), op=ALU.subtract)
                    if st is SELF:
                        i = v.tensor_tensor(out=zn_lo[:, kp, :, :], in0=z[:, bass.ds(b * QT, QT), :],
                                            in1=zn_hi[:, kp, :, :].bitcast(F32), op=ALU.subtract)
                    i.then_inc(s["zlo_done"], 1)

                def prep(b, kp, groups):
                    if st is SELF:
                        z_parts(b, kp)
                        return
                    for n in groups:
                        if n == 0:
                            z_parts(b, kp)
                        dve.wait_ge(s["chi_done"], b * 4 + n + 1)
                        cols = slice(CGROUPS[n][0] * P, CGROUPS[n][0] * P + width(n))
                        i = v.tensor_tensor(out=ct_lo[0:DC, kp, cols], in0=mx_ps[n % 2][0:DC, 0:width(n)],
                                        in1=ct_hi[0:DC, kp, cols].bitcast(F32), op=ALU.subtract)
                        if n == len(CGROUPS) - 1:
                            i = v.tensor_copy(ct_hi[0:DC, kp, sh.SK:sh.SK + 1], mx_ps[n % 2][0:DC, width(n) - 1:width(n)])
                        i.then_inc(s["mx_read"], 1)

                def queries(pr):
                    k = pr.hp % st.nq
                    dve.wait_ge(s["qhi_done"], pr.g + 1)
                    v.tensor_tensor(out=q_lo[0:st.qrows, k, :], in0=m_ps[0:st.qrows, :],
                                    in1=q_hi[0:st.qrows, k, :].bitcast(F32), op=ALU.subtract).then_inc(s["qlo_done"], 1)

                def maxima(pr, groups):
                    k = pr.hp % st.nq
                    for n in groups:
                        dve.wait_ge(s["mx_ready"], mx_count(st, pr) + n + 1)
                        if n == 0:
                            dve.wait_ge(s["mrow_in"][k], count(pr.g // st.nq * 64))
                        if st is SELF:
                            src = mx_ps[n % 2][:].rearrange("p (j k) -> p j k", j=QT)
                            v.tensor_reduce(negm[:, k, QT * n:QT * n + QT], src, AX.X, ALU.max,
                                            negate=True).then_inc(s["mx_read"], 1)
                        else:
                            v.tensor_reduce(mxp[:, k, n // 4, n % 4:n % 4 + 1], mx_ps[n % 2][:, 0:MXW[n % 4]],
                                            AX.X, ALU.max).then_inc(s["mx_read"], 1)
                    if st is CROSS and n == st.mx_groups - 1:
                        dve.wait_ge(s["mx_read"], mx_count(st, pr) + n + 1)
                        v.tensor_reduce(negm[:, k, :], mxp[:, k], AX.X, ALU.max, negate=True).then_inc(s["negm_ready"], 1)

                def output(b, g):
                    dve.wait_ge(s["out_ready"], g + 1)
                    for hh, bank in enumerate((o_ps, m_ps)):
                        den = bank[:, 0:QT * (D + 2)].rearrange("p (j c) -> p j c", j=QT)[:, :, D:D + 1]
                        v.reciprocal(rden[:, QT * hh:QT * hh + QT].rearrange("p (j o) -> p j o", o=1), den).then_inc(s["rden_made"], 1)
                    dve.wait_ge(s["rden_made"], 2 * g + 2)
                    dve.wait_ge(s["out_read"], count(g))
                    for hh, bank in enumerate((o_ps, m_ps)):
                        if hh:
                            dve.wait_ge(s["half_added"], g + 1)
                        for j in range(QT):
                            slab = xs[:, bass.ds(b * QT + j, 1), :].rearrange("p o d -> p (o d)")
                            i = v.scalar_tensor_tensor(
                                out=slab, in0=bank[:, j * (D + 2):j * (D + 2) + D], scalar=rden[:, QT * hh + j:QT * hh + j + 1],
                                in1=slab, op0=ALU.mult, op1=ALU.add)
                        i.then_inc(s["half_added"] if hh == 0 else s["out_read"], 1)

                def body(pr, last):
                    steps, nxt = plan(st, pr, last)
                    for t in range(st.nt):
                        r, k = pr.g * st.nt + t, st.bank(pr.hp, t)
                        kr = st.krows[t]
                        dve.wait_ge(s["exp_done"], r + 1)
                        v.tensor_tensor(out=p_lo[0:kr, k, :], in0=p_32[0:kr, k, :], in1=p_hi[0:kr, k, :].bitcast(F32),
                                        op=ALU.subtract).then_inc(s["plo_done"], 1)
                        for what, arg in steps[t]:
                            if what == "prep":
                                prep(pr.b + 1, (pr.bs + 1) % 2, arg)
                            if what == "q":
                                queries(nxt)
                            if what == "mx":
                                maxima(nxt, arg)
                            if what == "out" and not (isinstance(pr.g, int) and pr.g == 0):
                                output(pr.b if pr.hp else pr.b - 1, pr.g - 1)

                prep(0, 0, range(4))
                for pr in ahead_pairs(st):
                    queries(pr)
                    maxima(pr, range(st.mx_groups))
                pairs(dve, st, body)
                output(B - 1, B * NP_ - 1)
                dve.wait_ge(s["out_read"], B * NP_)

            def feed_forward():
                for k in range(2):
                    dve.wait_ge(w_hi, 8 + k + 1)
                    cols = slice(k * 512, (k + 1) * 512)
                    v.tensor_tensor(out=w1_lo[:, cols], in0=fill_bank(2 * NWG + k)[:], in1=w1_hi[:, cols].bitcast(F32),
                                    op=ALU.subtract).then_inc(w_out, 1)
                layer_norm(2)
                dve.wait_ge(bias_added, 12)
                for c in range(4):
                    dve.wait_ge(ffz_hi, c + 1)
                    v.tensor_tensor(out=q_lo[:, c % 2, :], in0=zt[:, c * 512:(c + 1) * 512],
                                    in1=q_hi[:, c % 2, :].bitcast(F32), op=ALU.subtract).then_inc(ffz_lo, 1)
                    dve.wait_ge(ff2_ready, count(c - 1))
                    for f in range(FC):
                        dve.wait_ge(gelu_done, FC * c + f + 1)
                        dve.wait_ge(ff1_ready, 2 * (FC * c + f) + 2)
                        v.scalar_tensor_tensor(out=ffx(c)[:, f * 512:(f + 1) * 512], in0=lin_ps[f % 2][:],
                                               scalar=bff1[:, f:f + 1], in1=p_32[:, f % 2, :],
                                               op0=ALU.add, op1=ALU.mult).then_inc(act_done, 1)
                    if c:
                        ff_add(c - 1)
                ff_add(3)

            def ff_add(c):
                dve.wait_ge(ff2_ready, c + 1)
                r = xs[:, 4 * c:4 * c + 4, :]
                v.tensor_tensor(out=r, in0=ff2_ps[c % 2][:].rearrange("p (j d) -> p j d", j=4), in1=r,
                                op=ALU.add).then_inc(ff_added, 1)

            make_mt()
            for n, st in enumerate(STAGES):
                if n == 0:
                    dve.wait_ge(x_in, 16)
                layer_norm(n)
                weights(n)
                dve.wait_ge(bias_added, 4 * n + 4)
                attention(st)
            feed_forward()

        @block.tensor
        def _(pe):
            mm = nc.tensor.matmul

            def three(dst, k_hi, k_lo, m_hi, m_lo, first=True, last=True):
                mm(dst, k_hi, m_hi, start=first, stop=False)
                mm(dst, k_hi, m_lo, start=False, stop=False)
                return mm(dst, k_lo, m_hi, start=False, stop=last)

            def weights(n):
                rows = P if n == 0 else DC
                pe.wait_ge(wts_in, 48 * (n + 1))
                pe.wait_ge(mt_made, 4)
                pe.wait_ge(consts, 3)
                if n:
                    pe.wait_ge(S["self"]["exp_done"], B * NP_ * QT)

                def bank_free(fill):
                    pe.wait_ge(w_out, count(fill - 2))

                for m in range(3):
                    r, c = (P, P) if m == 0 else (rows, rows)
                    by = (mt[:, (0, 1, 0)[m], :] if n == 0 else mt[:, 2, :] if m == 0 else ident[0:DC, 0:DC])
                    for k in range(2):
                        fill = NWG * n + 2 * m + k
                        bank_free(fill)
                        for i in range(4):
                            ins = mm(fill_view(fill, c)[:, i, :], raw[0:r, m, (4 * k + i) * P:(4 * k + i + 1) * P], by,
                                     start=True, stop=True)
                        ins.then_inc(w_ready, 1)
                pe.wait_ge(wo_in, 16 * (n + 1))
                for what in ("a", "b"):
                    for k in range(4):
                        odd, half = k // 2, k % 2
                        fill = NWG * n + (6 if what == "a" else 10) + k
                        bank_free(fill)
                        pe.wait_ge(w_out, NWG * n + 6)
                        r = slice(64 * odd, 64 * odd + 64)
                        for i in range(4):
                            c = 4 * half + i
                            if what == "a":
                                ins = mm(fill_view(fill, rows)[:, i, :], wt[r, 0, c, :], wt[r, 1, c, 0:rows],
                                         start=True, stop=True)
                            else:
                                ins = mm(fill_view(fill, D, rows)[:, i, :], wt[r, 2, c, 0:rows], wo[r, c, :],
                                         start=True, stop=True)
                        ins.then_inc(w_ready, 1)

            def layer_norm(n):
                for c in range(4):
                    pe.wait_ge(z_made, 4 * n + c + 1)
                    if c > 1:
                        pe.wait_ge(zt_copied, count(4 * n + c - 1))
                    bank = o_ps if c % 2 == 0 else m_ps
                    for i in range(4):
                        ins = nc.tensor.transpose(bank[:, i * P:(i + 1) * P], z[:, 4 * c + i, :], ident[:])
                    ins.then_inc(zt_ready, 1)

            def attention(st):
                s = S[st.name]

                def key_parts(kp, t):
                    if st is SELF:
                        c = slice(t * P, (t + 1) * P)
                        return zt_hi[:, kp, c], zt_lo[:, kp, c]
                    c = slice(t * P, t * P + st.krows[t])
                    return ct_hi[:, kp, c], ct_lo[0:DC, kp, c]

                def prep(b, kp, groups):
                    if st is SELF:
                        return
                    for n in groups:
                        if n == 0:
                            pe.wait_ge(ctx_in, (b + 1) * 32)
                        fill = b * (16 * NP_ + 4) + n
                        pe.wait_ge(s["mx_read"], count(fill - 1))
                        for t in CGROUPS[n]:
                            kr, o = st.krows[t], (t - CGROUPS[n][0]) * P
                            ins = nc.tensor.transpose(mx_ps[n % 2][0:DC, o:o + kr], craw[0:kr, t, :], ident[0:kr, 0:kr])
                        ins.then_inc(s["mx_ready"], 1)

                def queries(pr):
                    kp = pr.bs % 2
                    if pr.hp < st.ahead:
                        pe.wait_ge(s["zlo_done"], pr.b + 1)
                    pe.wait_ge(s["qlo_done"], count(pr.g))
                    back = pr.g - st.ahead - 1
                    pe.wait_ge(s["out_read"], count(back))
                    for hh in range(PAIR):
                        dst = m_ps[0:st.qrows, hh * SQ:(hh + 1) * SQ]
                        h = pr.hp * PAIR + hh
                        ah, al = a_hi[:, h, 0:st.qrows], a_lo[:, h, 0:st.qrows]
                        zh, zl = zt_hi[:, kp, :], zt_lo[:, kp, :]
                        ins = three(dst, ah, al, zh, zl)
                    ins.then_inc(s["q_ready"], 1)

                def maxima(pr, groups):
                    kp, k = pr.bs % 2, pr.hp % st.nq
                    for n in groups:
                        if n == 0:
                            pe.wait_ge(s["qhi_done"], pr.g + 1)
                            if st is CROSS:
                                pe.wait_ge(s["mx_read"], mx_count(st, Pair(pr.b, 0, 0, NP_)))
                        pe.wait_ge(s["mx_read"], count(mx_count(st, pr) + n - 1))
                        if st is SELF:
                            for j in range(QT):
                                c = (QT * n + j) * P
                                ins = mm(mx_ps[n % 2][:, j * SQ:(j + 1) * SQ], q_hi[:, k, c:c + P], zt_hi[:, kp, :],
                                         start=True, stop=True)
                        else:
                            c, x0, xw = n // 4 * P, MX0[n % 4], MXW[n % 4]
                            ins = mm(mx_ps[n % 2][:, 0:xw], q_hi[0:DC, k, c:c + P], ct_hi[0:DC, kp, x0:x0 + xw],
                                     start=True, stop=True)
                        ins.then_inc(s["mx_ready"], 1)

                def scores(pr, t):
                    kp, k, kr = pr.bs % 2, pr.hp % st.nq, st.krows[t]
                    if t == 0:
                        pe.wait_ge(s["mrow_in"][k], (pr.g // st.nq + 1) * 64)
                        pe.wait_ge(s["qlo_done"], pr.g + 1)
                    d = st.back(pr.hp, t)
                    if d <= 3:
                        pe.wait_ge(s["exp_done"], count(pr.g * st.nt + t - d + 1))
                    dst = s_ps[st.bank(pr.hp, t)][0:kr, :]
                    kh, kl = key_parts(kp, t)
                    r = st.drows
                    mm(dst, kh, q_hi[0:r, k, :], start=True, stop=False)
                    mm(dst, kh[0:st.qrows], q_lo[0:st.qrows, k, :], start=False, stop=False)
                    mm(dst, kl, q_hi[0:st.qrows, k, :], start=False, stop=True).then_inc(s["scores_ready"], 1)

                def values(pr, t):
                    kp, k, kr = pr.bs % 2, st.bank(pr.hp, t), st.krows[t]
                    if t == 0:
                        pe.wait_ge(s["u_copied"], count(pr.g))
                        if st is CROSS and pr.hp == 0:
                            pe.wait_ge(s["vlo_done"], 2 * pr.b + 2)
                    pe.wait_ge(s["plo_done"], pr.g * st.nt + t + 1)
                    if st is SELF:
                        vh, vl = zn_hi[:, kp, t, :], zn_lo[:, kp, t, :]
                    else:
                        vh, vl = cn_hi[0:kr, kp, t, 0:DC + 1], cn_lo[0:kr, kp, t, 0:DC + 1]
                    three(u_ps[0:st.drows, :], vh, vl, p_hi[0:kr, k, :], p_lo[0:kr, k, :],
                          t == 0, t == st.nt - 1).then_inc(s["pv_done"], 1)

                def outputs(g, hp, n_queries):
                    pe.wait_ge(s["u_copied"], g + 1)
                    pe.wait_ge(s["out_read"], count(g))
                    pe.wait_ge(s["qlo_done"], n_queries)
                    for hh, bank in enumerate((o_ps, m_ps)):
                        h = hp * PAIR + hh
                        for j in range(QT):
                            c = hh * SQ + j * P
                            ins = mm(bank[:, j * (D + 2):(j + 1) * (D + 2)], u_sb[0:st.drows, c:c + P], bm[0:st.drows, h, :],
                                     start=True, stop=True)
                    ins.then_inc(s["out_ready"], 1)

                def body(pr, last):
                    steps, nxt = plan(st, pr, last)
                    one = pr.next(1, last)
                    for t in range(st.nt):
                        if t + 2 < st.nt:
                            scores(pr, t + 2)
                        elif one:
                            scores(one, t + 2 - st.nt)
                        for what, arg in steps[t]:
                            if what == "prep":
                                prep(pr.b + 1, (pr.bs + 1) % 2, arg)
                            if what == "q":
                                queries(nxt)
                            if what == "mx":
                                maxima(nxt, arg)
                            if what == "out" and not (isinstance(pr.g, int) and pr.g == 0):
                                outputs(pr.g - 1, (pr.hp - 1) % NP_, nxt.g + 1 if nxt else B * NP_)
                        values(pr, t)

                prep(0, 0, range(4))
                for pr in ahead_pairs(st):
                    queries(pr)
                    maxima(pr, range(st.mx_groups))
                first = Pair(0, 0, 0, NP_)
                for t in range(2):
                    scores(first, t)
                pairs(pe, st, body)
                outputs(B * NP_ - 1, NP_ - 1, B * NP_)

            for n, st in enumerate(STAGES):
                if n:
                    pe.wait_ge(S["self"]["out_read"], B * NP_)
                weights(n)
                layer_norm(n)
                pe.wait_ge(zt_copied, 4 * n + 4)
                pe.wait_ge(w_out, NWG * (n + 1))
                attention(st)

            pe.wait_ge(ff_in, 32)
            pe.wait_ge(S["cross"]["exp_done"], B * NP_ * CT)
            for k in range(2):
                mm(fill_bank(2 * NWG + k)[:], mt[:, 3, :], raw[:, 0, k * 512:(k + 1) * 512],
                   start=True, stop=True).then_inc(w_ready, 1)
            pe.wait_ge(S["cross"]["out_read"], B * NP_)
            layer_norm(2)
            pe.wait_ge(w_out, 2 * NWG + 2)

            def second(c):
                pe.wait_ge(act_done, FC * (c + 1))
                pe.wait_ge(ff_added, count(c - 1))
                for j in range(4):
                    for f in range(FC):
                        ins = mm(ff2_ps[c % 2][:, j * D:(j + 1) * D], ffx(c)[:, f * 512 + j * P:f * 512 + (j + 1) * P],
                                 w2[:, f, :], start=f == 0, stop=f == FC - 1)
                ins.then_inc(ff2_ready, 1)

            for c in range(4):
                pe.wait_ge(ffz_lo, c + 1)
                for f in range(FC):
                    pe.wait_ge(act_done, count(FC * c + f - 1))
                    for bank, col in ((gate_ps[f % 2], (FC + f) * P), (lin_ps[f % 2], f * P)):
                        three(bank[:], w1_hi[:, col:col + P], w1_lo[:, col:col + P], q_hi[:, c % 2, :],
                              q_lo[:, c % 2, :]).then_inc(ff1_ready, 1)
                if c:
                    second(c - 1)
            second(3)


_NAMES = ("wq1", "wk1", "wv1", "wo1", "bo1", "g1", "b1", "wq2", "wk2", "wv2", "wo2", "bo2", "g2", "b2",
          "w_ff1", "b_ff1", "w_ff2", "b_ff2", "g3", "b3")


def kernel(**inputs):
    import numpy as np
    import concourse.bacc as bacc
    from concourse.bass_utils import run_bass_kernel_spmd

    nc = bacc.Bacc("TRN2", target_bir_lowering=False, num_devices=1)
    arrays, aps = {}, {}
    for name in ("x", "ctx_768") + tuple(f"L0_xattn_{n}" for n in _NAMES):
        a = np.ascontiguousarray(inputs[name])
        arrays[f"in_{name}"] = a
        aps[name] = nc.dram_tensor(f"in_{name}", a.shape, mybir.dt.from_np(a.dtype), kind="ExternalInput").ap()
    out = nc.dram_tensor("out", inputs["x"].shape, F32, kind="ExternalOutput").ap()
    build(nc, aps["x"], aps["ctx_768"], {n: aps[f"L0_xattn_{n}"] for n in _NAMES}, out)
    r = run_bass_kernel_spmd(nc, [arrays], core_ids=[0])
    return r.results[0]["out"]
```

```python
from contextlib import ExitStack

import concourse.bass as bass
from concourse import mybir

F32 = mybir.dt.float32
F32R = mybir.dt.float32r
ACT = mybir.ActivationFunctionType
ALU = mybir.AluOpType
AX = mybir.AxisListType

P = 128
AUG = 96
EPS = 1e-5
PAIR = 2
NSB = 3
NPS = 4
LEAD_PE = 3
LEAD_ACT = 2
LEAD_DVE = 1


class Shapes:
    def __init__(self, x, ctx, wq, wff1):
        self.B, self.SQ, self.D = x.shape
        _, self.SK, self.DC = ctx.shape
        self.HD = wq.shape[1]
        self.DH = 64
        self.H = self.HD // self.DH
        self.NP = self.H // PAIR
        self.QT = self.SQ // P
        self.W = PAIR * self.SQ
        self.NSLAB = self.B * self.QT
        self.HC = self.HD // P
        self.FF = wff1.shape[1] // 2
        self.FC = self.FF // P
        self.CT = -(-self.SK // P)
        self.CLAST = self.SK - (self.CT - 1) * P
        assert self.D == P and self.DC == AUG and self.W == 512 and self.SQ == 256
        assert self.NP == 8 and self.B == 8 and self.CLAST > 64 and self.CT % 2


def count(value):
    return max(value, 0) if isinstance(value, int) else value


class Stage:

    def __init__(self, name, nt, krows, drows, qrows, ahead, nq, mx_groups, mx_per_batch, ring):
        self.name = name
        self.nt = nt
        self.krows = krows
        self.drows = drows
        self.qrows = qrows
        self.ahead = ahead
        self.nq = nq
        self.mx_groups = mx_groups
        self.mx_per_batch = mx_per_batch
        self.ring = ring

    def bank(self, hp, t):
        return self.ring[(hp * self.nt + t) % len(self.ring)]

    def slot(self, hp, t):
        return (hp * self.nt + t) % NPS

    def back(self, hp, t):
        n, i = len(self.ring), hp * self.nt + t
        return next(k for k in range(1, n + 1) if self.ring[(i - k) % n] == self.ring[i % n])


class Pair:

    def __init__(self, b, bs, hp, np_):
        self.b, self.bs, self.hp, self.np_ = b, bs, hp, np_
        self.g = b * np_ + hp

    def next(self, n, last_b):
        if self.hp + n < self.np_:
            return Pair(self.b, self.bs, self.hp + n, self.np_)
        if last_b:
            return None
        return Pair(self.b + 1, self.bs + 1, self.hp + n - self.np_, self.np_)


def build(nc, x, ctx, w, out):
    sh = Shapes(x, ctx, w["wq1"], w["w_ff1"])
    B, SQ, D, H, NP_, QT, W, CT, DC = sh.B, sh.SQ, sh.D, sh.H, sh.NP, sh.QT, sh.W, sh.CT, sh.DC
    NSLAB, HC, FC, HD = sh.NSLAB, sh.HC, sh.FC, sh.HD
    SCALE = float(sh.DH) ** -0.5
    SKP = CT * P
    MXW = [402, 400, 400, 400]
    MX0 = [0, 402, 802, 1202]
    assert MX0[-1] + MXW[-1] == sh.SK + sh.SK % 2

    SELF = Stage("self", QT, [P] * QT, P, P, 4, 4, 2, 0, [0, 1, 2, 0, 1, 2, 0, 1])
    CROSS = Stage("cross", CT, [P] * (CT - 1) + [sh.CLAST], DC + 1, DC, 2, 4, 16, 4,
                  [t % NSB for t in range(CT)] + [(t + 1) % NSB for t in range(CT)])
    STAGES = (SELF, CROSS)

    with ExitStack() as stack:
        stack.enter_context(nc.allow_non_contiguous_dma(reason="columns of at most 512 values"))

        def sb(name, shape, dt=F32):
            return stack.enter_context(nc.sbuf_tensor(name, shape, dt))

        def sem(name):
            return stack.enter_context(nc.semaphore(name))

        xs = sb("xs", [P, NSLAB, D])
        z = sb("z", [P, NSLAB, D])
        zt = sb("zt", [P, NSLAB * P])
        stats = sb("stats", [P, NSLAB, 6])
        mv = sb("mv", [P, NSLAB, 2])
        veps = sb("veps", [P, NSLAB])
        rstd = sb("rstd", [P, NSLAB])
        mhalf = sb("mhalf", [P, NSLAB])
        zeros = sb("zeros", [P, CT, 1])
        ident = sb("ident", [P, P])
        fold = sb("fold", [P, P])
        gcol = sb("gcol", [P, 3])
        bcol = sb("bcol", [P, 3])
        mt = sb("mt", [P, 4, P])
        bo = sb("bo", [P, 3, D])
        bff1 = sb("bff1", [P, 2 * FC])
        raw = sb("raw", [P, 3, HD])
        wo = sb("wo", [P, HC, D])
        wt = sb("wt", [P, 3, HC, P])
        a_hi = sb("a_hi", [P, H, P], F32R)
        a_lo = sb("a_lo", [P, H, P], F32R)
        bm = sb("bm", [P, H, D + 2])
        zt_hi = sb("zt_hi", [P, 2, SQ], F32R)
        zt_lo = sb("zt_lo", [P, 2, SQ], F32R)
        zn_hi = sb("zn_hi", [P, 2, QT, P], F32R)
        zn_lo = sb("zn_lo", [P, 2, QT, P], F32R)
        craw = sb("craw", [P, CT, DC])
        ct_hi = sb("ct_hi", [DC + 1, 2, SKP], F32R)
        ct_lo = sb("ct_lo", [DC + 1, 2, SKP], F32R)
        cn_hi = sb("cn_hi", [P, 2, CT, DC + 2], F32R)
        cn_lo = sb("cn_lo", [P, 2, CT, DC + 2], F32R)
        q_hi = sb("q_hi", [P, 4, W], F32R)
        q_lo = sb("q_lo", [P, 4, W], F32R)
        p_32 = sb("p_32", [P, NPS, W])
        p_hi = sb("p_hi", [P, NPS, W], F32R)
        p_lo = sb("p_lo", [P, NPS, W], F32R)
        mxp = sb("mxp", [P, 4, 4, 4])
        negm = sb("negm", [P, 4, 4], F32R)
        u_sb = sb("u_sb", [P, 2, W])
        rden = sb("rden", [P, 4])
        o_sum = sb("o_sum", [P, QT, D])
        o_sb = sb("o_sb", [P, PAIR, QT, D])
        w1_hi = sb("w1_hi", [P, 2 * sh.FF], F32R)
        w1_lo = sb("w1_lo", [P, 2 * sh.FF], F32R)
        w2 = sb("w2", [P, FC, D])

        banks = [stack.enter_context(nc.psum_tensor(f"bank{i}", [P, 512], F32)) for i in range(8)]
        s_ps = banks[0:3]
        u_ps = banks[3]
        mx_ps = banks[4:6]
        o_ps = banks[6]
        m_ps = banks[7]
        mx_banks = {SELF: mx_ps[0:1], CROSS: mx_ps}
        q_bank = {SELF: mx_ps[1], CROSS: m_ps}

        x_in, wts_in, small_in, consts, ctx_in, stored = (
            sem(n) for n in ("x_in", "wts_in", "small_in", "consts", "ctx_in", "stored"))
        wo_in, ff_in = sem("wo_in"), sem("ff_in")
        var_ready, rstd_made = sem("var_ready"), sem("rstd_made")
        mt_made, ln_step, z_made, zt_ready, zt_copied, bias_added = (
            sem(n) for n in ("mt_made", "ln_step", "z_made", "zt_ready", "zt_copied", "bias_added"))
        w_ready, w_hi, w_out, bm_set, ones_set, mt_step = (
            sem(n) for n in ("w_ready", "w_hi", "w_out", "bm_set", "ones_set", "mt_step"))
        S = {}
        for st in STAGES:
            S[st.name] = {n: sem(f"{st.name}_{n}") for n in (
                "scores_ready", "exp_done", "plo_done", "pv_done", "q_ready", "qhi_done", "qlo_done",
                "mx_ready", "mx_read", "negm_ready", "u_copied", "out_ready", "rden_made",
                "out_read", "half_added", "pair_added", "batch_added", "zhi_done", "zlo_done", "chi_done", "vhi_done",
                "vlo_done")}
        for st in STAGES:
            S[st.name]["mrow_in"] = [sem(f"{st.name}_mrow_in{k}") for k in range(st.nq)]
        ff1_ready, gelu_done, act_done, ff2_ready, ff_added = (
            sem(n) for n in ("ff1_ready", "gelu_done", "act_done", "ff2_ready", "ff_added"))
        ffz_hi, ffz_lo = sem("ffz_hi"), sem("ffz_lo")

        def pairs(eng, st, body):
            def batch(b, bs, last):
                for hp in range(NP_):
                    body(Pair(b, bs, hp, NP_), last)

            batch(0, 0, False)
            with eng.Fori(0, (B - 2) // 2) as i:
                for k in range(2):
                    batch(i * 2 + (1 + k), 1 + k, False)
            batch(B - 1, B - 1, True)

        def ahead_pairs(st):
            return [Pair(0, 0, n, NP_) for n in range(st.ahead)]

        def tile_ahead(st, pr, t, n, last):
            nxt = pr.next((t + n) // st.nt, last)
            return (nxt, (t + n) % st.nt) if nxt else None

        def first_tiles(st, n):
            return [(Pair(0, 0, i // st.nt, NP_), i % st.nt) for i in range(n)]

        def needs_prep(st, pr, last):
            return not last and pr.hp + st.ahead == NP_

        def mx_count(st, pr):
            return pr.g * st.mx_groups + (pr.b + 1) * st.mx_per_batch

        def plan(st, pr, last):
            steps = [[] for _ in range(st.nt)]
            nxt = pr.next(st.ahead, last)
            prep = nxt and needs_prep(st, pr, last)
            if st is SELF:
                if prep:
                    steps[0].append(("prep", range(1)))
                before = pr.next(st.ahead - 1, last)
                if before:
                    steps[0].append(("mx", (before, range(1, 2))))
                if nxt:
                    steps[0].append(("q", None))
                steps[0].append(("scale", 2))
                if nxt:
                    steps[1].append(("mx", (nxt, range(0, 1))))
                steps[1].append(("out", None))
                return steps, nxt
            if prep:
                for k in range(4):
                    steps[k].append(("prep", range(k, k + 1)))
            if nxt:
                steps[0].append(("q", None))
                n0 = 4 if prep else 1
                left = CT - n0
                for k in range(left):
                    steps[n0 + k].append(("mx", (nxt, range(16 * k // left, 16 * (k + 1) // left))))
            steps[2].append(("out", None))
            steps[3].append(("scale", 1))
            return steps, nxt

        CGROUPS = [range(0, 4), range(4, 8), range(8, 12), range(12, CT)]
        NWG = 14

        def width(n):
            return (len(CGROUPS[n]) - 1) * P + (sh.CLAST if n == len(CGROUPS) - 1 else P)

        def heads(t, half, odd, c):
            return t[:, 8 * half + odd:8 * half + odd + 7:2, 0:c]

        def fill_bank(fill):
            return s_ps[fill % NSB]

        def fill_view(fill, c, rows=P):
            return fill_bank(fill)[0:rows, 0:4 * c].rearrange("p (h c) -> p h c", h=4)

        gate_ps = [s_ps[0], mx_ps[0]]
        lin_ps = [s_ps[1], mx_ps[1]]
        ff2_ps = [s_ps[2], u_ps]

        def ffx(c):
            t = wt[:, 0:2].rearrange("p a c d -> p (a c d)") if c % 2 == 0 else raw[:, 1:3].rearrange("p a c -> p (a c)")
            return t

        block = stack.enter_context(nc.Block())

        def load_context(sp, b):
            full = (CT - 1) * P
            one = isinstance(b, int)
            src = ctx[b] if one else ctx[bass.ds(b, 1)].rearrange("o s d -> (o s) d")
            sp.dma_start(craw[:, 0:CT - 1, :], src[0:full, :].rearrange("(t p) d -> p t d", p=P)).then_inc(ctx_in, 16)
            sp.dma_start(craw[0:sh.CLAST, CT - 1, :], src[full:sh.SK, :]).then_inc(ctx_in, 16)

        def mrows(sp, st):
            s = S[st.name]

            def row(pr):
                if st is SELF:
                    sp.wait_ge(s["mx_read"], mx_count(st, pr) + st.mx_groups)
                else:
                    sp.wait_ge(s["negm_ready"], pr.g + 1)
                q = pr.hp % st.nq
                for j in range(4):
                    sp.dma_start(q_hi[AUG:AUG + 1, q, j * P:(j + 1) * P].bitcast(F32),
                                 negm[:, q, j:j + 1].bitcast(F32)).then_inc(s["mrow_in"][q], 16)

            def body(pr, last):
                if st is CROSS and pr.hp == 0 and not last:
                    sp.wait_ge(s["vlo_done"], 2 * pr.b + 2)
                    sp.wait_ge(s["mx_ready"], (pr.b + 1) * 4 + pr.b * 128)
                    load_context(sp, pr.b + 1)
                nxt = pr.next(st.ahead, last)
                if nxt:
                    row(nxt)

            for pr in ahead_pairs(st):
                row(pr)
            pairs(sp, st, body)

        @block.sync
        def _(sp):
            sp.dma_start(xs[:], x.rearrange("b (t p) d -> p (b t) d", p=P)).then_inc(x_in, 16)
            for i in (1, 2, 3):
                sp.dma_start(gcol[:, i - 1:i], w[f"g{i}"].rearrange("(p o) -> p o", o=1)).then_inc(small_in, 16)
                sp.dma_start(bcol[:, i - 1:i], w[f"b{i}"].rearrange("(p o) -> p o", o=1)).then_inc(small_in, 16)
            for i, n in enumerate(("wq1", "wk1", "wv1")):
                sp.dma_start(raw[:, i, :], w[n]).then_inc(wts_in, 16)
            sp.dma_start(wo[:], w["wo1"].rearrange("(c p) d -> p c d", p=P)).then_inc(wo_in, 16)
            for i, n in enumerate(("bo1", "bo2", "b_ff2")):
                sp.dma_start(bo[:, i, :], w[n].rearrange("(o d) -> o d", o=1).to_broadcast([P, D])).then_inc(small_in, 16)
            sp.dma_start(bff1[:], w["b_ff1"].rearrange("(c p) -> p c", p=P)).then_inc(small_in, 16)
            load_context(sp, 0)
            mrows(sp, SELF)
            sp.wait_ge(w_out, NWG)
            for i, n in enumerate(("wq2", "wk2", "wv2")):
                sp.dma_start(raw[0:w[n].shape[0], i, :], w[n]).then_inc(wts_in, 16)
            sp.dma_start(wo[:], w["wo2"].rearrange("(c p) d -> p c d", p=P)).then_inc(wo_in, 16)
            sp.wait_ge(w_out, 2 * NWG)
            sp.dma_start(raw[:, 0, :], w["w_ff1"]).then_inc(ff_in, 16)
            sp.dma_start(w2[:], w["w_ff2"].rearrange("(c p) d -> p c d", p=P)).then_inc(ff_in, 16)
            mrows(sp, CROSS)
            for c in range(4):
                sp.wait_ge(ff_added, c + 1)
                sp.dma_start(out.rearrange("b (t p) d -> p (b t) d", p=P)[:, 4 * c:4 * c + 4, :],
                             xs[:, 4 * c:4 * c + 4, :]).then_inc(stored, 16)
            sp.wait_ge(stored, 4 * 16)

        def split_context(pool, b, kp):
            s = S["cross"]
            pool.wait_ge(ctx_in, (b + 1) * 32)
            for n, (hi, t0, t1) in enumerate(((P, 0, CT - 1), (sh.CLAST, CT - 1, CT))):
                pool.wait_ge(s["vlo_done"], 2 * b + n)
                nc.gpsimd.tensor_tensor(out=cn_hi[0:hi, kp, t0:t1, 0:DC], in0=craw[0:hi, t0:t1, :],
                                        in1=zeros[0:hi, 0:t1 - t0, 0:1].to_broadcast([hi, t1 - t0, DC]),
                                        op=ALU.add).then_inc(s["vhi_done"], 1)
                pool.wait_ge(s["vhi_done"], 2 * b + n + 1)
                nc.gpsimd.tensor_tensor(out=cn_lo[0:hi, kp, t0:t1, 0:DC], in0=craw[0:hi, t0:t1, :],
                                        in1=cn_hi[0:hi, kp, t0:t1, 0:DC].bitcast(F32),
                                        op=ALU.subtract).then_inc(s["vlo_done"], 1)

        @block.gpsimd
        def _(pool):
            g = nc.gpsimd

            def add_pairs(st):
                s = S[st.name]
                if st is CROSS:
                    split_context(pool, 0, 0)

                def body(pr, last):
                    if st is CROSS and needs_prep(st, pr, last):
                        if not (isinstance(pr.b, int) and pr.b == 0):
                            pool.wait_ge(s["pv_done"], pr.b * (NP_ * CT))
                        split_context(pool, pr.b + 1, (pr.bs + 1) % 2)
                    pool.wait_ge(s["out_read"], pr.g + 1)
                    if pr.hp == 0:
                        if not (isinstance(pr.b, int) and pr.b == 0):
                            pool.wait_ge(s["batch_added"], pr.b)
                        g.tensor_tensor(out=o_sum[:], in0=o_sb[:, 0], in1=o_sb[:, 1], op=ALU.add).then_inc(s["pair_added"], 1)
                        return
                    pool.wait_ge(s["pair_added"], pr.g)
                    g.tensor_tensor(out=o_sum[:], in0=o_sb[:, 0], in1=o_sum[:], op=ALU.add).then_inc(s["half_added"], 1)
                    pool.wait_ge(s["half_added"], pr.b * (NP_ - 1) + pr.hp)
                    g.tensor_tensor(out=o_sum[:], in0=o_sb[:, 1], in1=o_sum[:], op=ALU.add).then_inc(s["pair_added"], 1)

                pairs(pool, st, body)

            g.memset(ident[:], 0.0).then_inc(consts, 1)
            pool.wait_ge(consts, 1)
            g.affine_select(out=ident[:], in_=ident[:], compare_op=ALU.not_equal, fill=1.0, base=0,
                            pattern=[[-1, P]], channel_multiplier=1).then_inc(consts, 1)
            pool.wait_ge(consts, 2)
            g.affine_select(out=fold[:], in_=ident[:], compare_op=ALU.not_equal, fill=-1.0, base=-AUG,
                            pattern=[[0, P]], channel_multiplier=1).then_inc(consts, 1)
            g.memset(mhalf[:], -0.5).then_inc(consts, 1)
            g.memset(zeros[:], 0.0).then_inc(consts, 1)
            g.memset(bm[:], 0.0).then_inc(bm_set, 1)
            pool.wait_ge(bm_set, 1)
            g.memset(bm[AUG:AUG + 1, :, D:D + 1], 1.0).then_inc(bm_set, 1)
            g.memset(ct_hi[AUG:AUG + 1].bitcast(F32), 1.0).then_inc(ones_set, 1)
            pool.wait_ge(ones_set, 1)
            g.memset(cn_hi[:, :, :, DC:DC + 2].bitcast(F32), 1.0).then_inc(ones_set, 1)
            g.memset(cn_lo[:, :, :, DC:DC + 2].bitcast(F32), 0.0).then_inc(ones_set, 1)
            pool.wait_ge(small_in, 10 * 16)
            for n in range(3):
                if n == 1:
                    pool.wait_ge(S["self"]["pair_added"], B * NP_)
                    g.memset(bm[AUG:AUG + 1, :, 0:D], 0.0).then_inc(bm_set, 1)
                    pool.wait_ge(bm_set, 3)
                for c in range(4):
                    cols = slice(4 * c, 4 * c + 4)
                    if c == 0:
                        pool.wait_ge(consts, 5)
                    pool.wait_ge(var_ready, 4 * n + c + 1)
                    g.tensor_tensor(out=rstd[:, cols], in0=veps[:, cols], in1=mhalf[:, cols],
                                    op=ALU.pow).then_inc(rstd_made, 1)
                    pool.wait_ge(z_made, 4 * n + c + 1)
                    v = xs[:, 4 * c:4 * c + 4, :]
                    g.tensor_tensor(out=v, in0=v, in1=bo[:, n:n + 1, :].to_broadcast([P, 4, D]),
                                    op=ALU.add).then_inc(bias_added, 1)
                if n < 2:
                    add_pairs(STAGES[n])

        @block.scalar
        def _(act):
            def copy(dst, src):
                return nc.scalar.activation(dst, src, ACT.Copy)

            def weights(n):
                for k in range(4):
                    fill = NWG * n + 6 + k
                    act.wait_ge(w_ready, fill + 1)
                    odd, half = k // 2, k % 2
                    c = P if n == 0 else DC
                    copy(heads(a_hi, half, odd, c), fill_view(fill, c)).then_inc(w_hi, 1)

            def layer_norm(n):
                for c in range(4):
                    act.wait_ge(zt_ready, 4 * n + c + 1)
                    copy(zt[:, c * 512:(c + 1) * 512], o_ps[:] if c % 2 == 0 else m_ps[:]).then_inc(zt_copied, 1)

            def attention(st):
                s = S[st.name]

                def z_parts(b, kp):
                    off = b * SQ
                    i = copy(zt_hi[:, kp, :], zt[:, bass.ds(off, SQ)])
                    if st is SELF:
                        i = copy(zn_hi[:, kp, :, :], z[:, bass.ds(b * QT, QT), :])
                    i.then_inc(s["zhi_done"], 1)

                def prep(b, kp, groups):
                    if st is SELF:
                        z_parts(b, kp)
                        return
                    for n in groups:
                        if n == 0:
                            z_parts(b, kp)
                        fill = b * (16 * NP_ + 4) + n
                        act.wait_ge(s["mx_ready"], fill + 1)
                        cols = slice(CGROUPS[n][0] * P, CGROUPS[n][0] * P + width(n))
                        copy(ct_hi[0:DC, kp, cols], mx_ps[n % 2][0:DC, 0:width(n)]).then_inc(s["chi_done"], 1)

                def queries(pr):
                    act.wait_ge(s["q_ready"], pr.g + 1)
                    copy(q_hi[0:st.qrows, pr.hp % st.nq, :], q_bank[st][0:st.qrows, :]).then_inc(s["qhi_done"], 1)

                def u_copy(g, k):
                    act.wait_ge(s["pv_done"], (g + 1) * st.nt)
                    act.wait_ge(s["out_ready"], count(g - 1))
                    copy(u_sb[0:st.drows, k, :], u_ps[0:st.drows, :]).then_inc(s["u_copied"], 1)

                def scale_out(g):
                    act.wait_ge(s["rden_made"], g + 1)
                    act.wait_ge(s["pair_added"], count(g))
                    for hh, bank in enumerate((o_ps, m_ps)):
                        for j in range(QT):
                            i = nc.scalar.activation(o_sb[:, hh, j, :], bank[:, j * (D + 2):j * (D + 2) + D], ACT.Copy,
                                                     scale=rden[:, QT * hh + j:QT * hh + j + 1])
                    i.then_inc(s["out_read"], 1)

                def exponentials(pr, t):
                    r, bank, k, kr = pr.g * st.nt + t, st.bank(pr.hp, t), st.slot(pr.hp, t), st.krows[t]
                    act.wait_ge(s["scores_ready"], r + 1)
                    act.wait_ge(s["pv_done"], count(r - NPS + 1))
                    nc.scalar.activation(p_32[0:kr, k, :], s_ps[bank][0:kr, :], ACT.Exp, scale=SCALE)
                    nc.scalar.activation(p_hi[0:kr, k, :], s_ps[bank][0:kr, :], ACT.Exp,
                                         scale=SCALE).then_inc(s["exp_done"], 1)

                def body(pr, last):
                    steps, nxt = plan(st, pr, last)
                    for t in range(st.nt):
                        if t == 0 and not (isinstance(pr.g, int) and pr.g == 0):
                            u_copy(pr.g - 1, (pr.hp - 1) % 2)
                        ahead = tile_ahead(st, pr, t, LEAD_ACT, last)
                        if ahead:
                            exponentials(*ahead)
                        for what, arg in steps[t]:
                            if what == "prep":
                                prep(pr.b + 1, (pr.bs + 1) % 2, arg)
                            if what == "q":
                                queries(nxt)
                            if what == "scale" and not (isinstance(pr.g, int) and pr.g < arg):
                                scale_out(pr.g - arg)

                prep(0, 0, range(4))
                for pr in ahead_pairs(st):
                    queries(pr)
                for pr, t in first_tiles(st, LEAD_ACT):
                    exponentials(pr, t)
                pairs(act, st, body)
                if st is SELF:
                    scale_out(B * NP_ - 2)
                u_copy(B * NP_ - 1, (NP_ - 1) % 2)
                scale_out(B * NP_ - 1)

            weights(0)
            layer_norm(0)
            act.wait_ge(zt_copied, 4)
            attention(SELF)
            weights(1)
            layer_norm(1)
            act.wait_ge(zt_copied, 8)
            attention(CROSS)
            for k in range(2):
                act.wait_ge(w_ready, 2 * NWG + k + 1)
                copy(w1_hi[:, k * 512:(k + 1) * 512], fill_bank(2 * NWG + k)[:]).then_inc(w_hi, 1)
            layer_norm(2)
            for c in range(4):
                act.wait_ge(zt_copied, 8 + c + 1)
                act.wait_ge(ff1_ready, count(8 * (c - 1)))
                copy(q_hi[:, c % 2, :], zt[:, c * 512:(c + 1) * 512]).then_inc(ffz_hi, 1)
                for f in range(FC):
                    act.wait_ge(ff1_ready, 8 * c + 2 * f + 1)
                    act.wait_ge(act_done, count(FC * c + f - 1))
                    nc.scalar.activation(p_32[:, f % 2, :], gate_ps[f % 2][:], ACT.Gelu,
                                         bias=bff1[:, FC + f:FC + f + 1]).then_inc(gelu_done, 1)

        @block.vector
        def _(dve):
            v = nc.vector

            def weights(n):
                rows = P if n == 0 else DC
                for m in range(3):
                    c = P if m == 0 else rows
                    for k in range(2):
                        fill = NWG * n + 2 * m + k
                        dve.wait_ge(w_ready, fill + 1)
                        v.tensor_copy(wt[:, m, 4 * k:4 * k + 4, 0:c], fill_view(fill, c)).then_inc(w_out, 1)
                for k in range(4):
                    fill = NWG * n + 6 + k
                    odd, half = k // 2, k % 2
                    dve.wait_ge(w_hi, 4 * n + k + 1)
                    v.tensor_tensor(out=heads(a_lo, half, odd, rows), in0=fill_view(fill, rows),
                                    in1=heads(a_hi, half, odd, rows).bitcast(F32), op=ALU.subtract).then_inc(w_out, 1)
                dve.wait_ge(bm_set, 2 + n)
                for k in range(4):
                    fill = NWG * n + 10 + k
                    odd, half = k // 2, k % 2
                    dve.wait_ge(w_ready, fill + 1)
                    v.tensor_copy(heads(bm, half, odd, D)[0:rows], fill_view(fill, D, rows)).then_inc(w_out, 1)

            def make_mt():
                dve.wait_ge(small_in, 160)
                dve.wait_ge(consts, 3)
                for k, i in enumerate((0, 0, 1, 2)):
                    v.tensor_scalar(mt[:, k, :], fold[:], gcol[:, i:i + 1], None, ALU.mult).then_inc(mt_step, 1)
                dve.wait_ge(mt_step, 4)
                for k, i in enumerate((0, None, 1, 2)):
                    col = mt[:, k, AUG:AUG + 1]
                    if i is None:
                        ins = v.memset(col, 0.0)
                    else:
                        ins = v.tensor_copy(col, bcol[:, i:i + 1])
                    ins.then_inc(mt_made, 1)

            def layer_norm(n):
                step = [ln_count[0]]

                def done(ins):
                    step[0] += 1
                    ins.then_inc(ln_step, 1)

                for c in range(4):
                    slabs = range(4 * c, 4 * c + 4)
                    if n:
                        dve.wait_ge(zt_ready, 4 * n)
                    for i in slabs:
                        done(v.bn_stats(stats[:, i, :], xs[:, i, :]))
                    dve.wait_ge(ln_step, step[0])
                    for i in slabs:
                        done(v.bn_aggr(mv[:, i, :], stats[:, i, :]))
                    dve.wait_ge(ln_step, step[0])
                    v.tensor_scalar(veps[:, 4 * c:4 * c + 4], mv[:, 4 * c:4 * c + 4, 1], EPS, None, ALU.add).then_inc(var_ready, 1)
                    dve.wait_ge(rstd_made, 4 * n + c + 1)
                    for i in slabs:
                        done(v.tensor_scalar(z[:, i, :], xs[:, i, :], mv[:, i, 0:1], rstd[:, i:i + 1],
                                             ALU.subtract, ALU.mult))
                    dve.wait_ge(ln_step, step[0])
                    v.memset(z[:, 4 * c:4 * c + 4, AUG:AUG + 1], 1.0).then_inc(z_made, 1)
                ln_count[0] = step[0]

            ln_count = [0]

            def attention(st):
                s = S[st.name]

                def z_parts(b, kp):
                    dve.wait_ge(s["zhi_done"], b + 1)
                    i = v.tensor_tensor(out=zt_lo[:, kp, :], in0=zt[:, bass.ds(b * SQ, SQ)],
                                        in1=zt_hi[:, kp, :].bitcast(F32), op=ALU.subtract)
                    if st is SELF:
                        i = v.tensor_tensor(out=zn_lo[:, kp, :, :], in0=z[:, bass.ds(b * QT, QT), :],
                                            in1=zn_hi[:, kp, :, :].bitcast(F32), op=ALU.subtract)
                    i.then_inc(s["zlo_done"], 1)

                def prep(b, kp, groups):
                    if st is SELF:
                        z_parts(b, kp)
                        return
                    for n in groups:
                        if n == 0:
                            z_parts(b, kp)
                        dve.wait_ge(s["chi_done"], b * 4 + n + 1)
                        cols = slice(CGROUPS[n][0] * P, CGROUPS[n][0] * P + width(n))
                        i = v.tensor_tensor(out=ct_lo[0:DC, kp, cols], in0=mx_ps[n % 2][0:DC, 0:width(n)],
                                        in1=ct_hi[0:DC, kp, cols].bitcast(F32), op=ALU.subtract)
                        if n == len(CGROUPS) - 1:
                            i = v.tensor_copy(ct_hi[0:DC, kp, sh.SK:sh.SK + 1], mx_ps[n % 2][0:DC, width(n) - 1:width(n)])
                        i.then_inc(s["mx_read"], 1)

                def queries(pr):
                    k = pr.hp % st.nq
                    dve.wait_ge(s["qhi_done"], pr.g + 1)
                    v.tensor_tensor(out=q_lo[0:st.qrows, k, :], in0=q_bank[st][0:st.qrows, :],
                                    in1=q_hi[0:st.qrows, k, :].bitcast(F32), op=ALU.subtract).then_inc(s["qlo_done"], 1)

                def maxima(pr, groups):
                    k = pr.hp % st.nq
                    for n in groups:
                        dve.wait_ge(s["mx_ready"], mx_count(st, pr) + n + 1)
                        if n == 0:
                            dve.wait_ge(s["mrow_in"][k], count(pr.g // st.nq * 64))
                        if st is SELF:
                            src = mx_banks[st][0][:].rearrange("p (j k) -> p j k", j=QT)
                            v.tensor_reduce(negm[:, k, QT * n:QT * n + QT], src, AX.X, ALU.max,
                                            negate=True).then_inc(s["mx_read"], 1)
                        else:
                            v.tensor_reduce(mxp[:, k, n // 4, n % 4:n % 4 + 1], mx_ps[n % 2][:, 0:MXW[n % 4]],
                                            AX.X, ALU.max).then_inc(s["mx_read"], 1)
                    if st is CROSS and n == st.mx_groups - 1:
                        dve.wait_ge(s["mx_read"], mx_count(st, pr) + n + 1)
                        v.tensor_reduce(negm[:, k, :], mxp[:, k], AX.X, ALU.max, negate=True).then_inc(s["negm_ready"], 1)

                def denominators(g):
                    dve.wait_ge(s["out_ready"], g + 1)
                    for hh, bank in enumerate((o_ps, m_ps)):
                        den = bank[:, 0:QT * (D + 2)].rearrange("p (j c) -> p j c", j=QT)[:, :, D:D + 1]
                        i = v.reciprocal(rden[:, QT * hh:QT * hh + QT].rearrange("p (j o) -> p j o", o=1), den)
                    i.then_inc(s["rden_made"], 1)

                def add_batch(b):
                    dve.wait_ge(s["pair_added"], (b + 1) * NP_)
                    rows = xs[:, bass.ds(b * QT, QT), :]
                    v.tensor_tensor(out=rows, in0=o_sum[:], in1=rows, op=ALU.add).then_inc(s["batch_added"], 1)

                def low_part(pr, t):
                    k, kr = st.slot(pr.hp, t), st.krows[t]
                    dve.wait_ge(s["exp_done"], pr.g * st.nt + t + 1)
                    v.tensor_tensor(out=p_lo[0:kr, k, :], in0=p_32[0:kr, k, :], in1=p_hi[0:kr, k, :].bitcast(F32),
                                    op=ALU.subtract).then_inc(s["plo_done"], 1)

                def body(pr, last):
                    steps, nxt = plan(st, pr, last)
                    for t in range(st.nt):
                        ahead = tile_ahead(st, pr, t, LEAD_DVE, last)
                        if ahead:
                            low_part(*ahead)
                        for what, arg in steps[t]:
                            if what == "prep":
                                prep(pr.b + 1, (pr.bs + 1) % 2, arg)
                            if what == "q":
                                queries(nxt)
                            if what == "mx":
                                maxima(*arg)
                            if what == "out" and not (isinstance(pr.g, int) and pr.g == 0):
                                if pr.hp == 1 and not (isinstance(pr.b, int) and pr.b == 0):
                                    add_batch(pr.b - 1)
                                denominators(pr.g - 1)

                prep(0, 0, range(4))
                for pr in ahead_pairs(st):
                    queries(pr)
                    if st is SELF and pr.hp == st.ahead - 1:
                        maxima(pr, range(1))
                    else:
                        maxima(pr, range(st.mx_groups))
                for pr, t in first_tiles(st, LEAD_DVE):
                    low_part(pr, t)
                pairs(dve, st, body)
                denominators(B * NP_ - 1)
                add_batch(B - 1)
                dve.wait_ge(s["batch_added"], B)

            def feed_forward():
                for k in range(2):
                    dve.wait_ge(w_hi, 8 + k + 1)
                    cols = slice(k * 512, (k + 1) * 512)
                    v.tensor_tensor(out=w1_lo[:, cols], in0=fill_bank(2 * NWG + k)[:], in1=w1_hi[:, cols].bitcast(F32),
                                    op=ALU.subtract).then_inc(w_out, 1)
                layer_norm(2)
                dve.wait_ge(bias_added, 12)
                for c in range(4):
                    dve.wait_ge(ffz_hi, c + 1)
                    v.tensor_tensor(out=q_lo[:, c % 2, :], in0=zt[:, c * 512:(c + 1) * 512],
                                    in1=q_hi[:, c % 2, :].bitcast(F32), op=ALU.subtract).then_inc(ffz_lo, 1)
                    dve.wait_ge(ff2_ready, count(c - 1))
                    for f in range(FC):
                        dve.wait_ge(gelu_done, FC * c + f + 1)
                        dve.wait_ge(ff1_ready, 2 * (FC * c + f) + 2)
                        v.scalar_tensor_tensor(out=ffx(c)[:, f * 512:(f + 1) * 512], in0=lin_ps[f % 2][:],
                                               scalar=bff1[:, f:f + 1], in1=p_32[:, f % 2, :],
                                               op0=ALU.add, op1=ALU.mult).then_inc(act_done, 1)
                    if c:
                        ff_add(c - 1)
                ff_add(3)

            def ff_add(c):
                dve.wait_ge(ff2_ready, c + 1)
                r = xs[:, 4 * c:4 * c + 4, :]
                v.tensor_tensor(out=r, in0=ff2_ps[c % 2][:].rearrange("p (j d) -> p j d", j=4), in1=r,
                                op=ALU.add).then_inc(ff_added, 1)

            make_mt()
            for n, st in enumerate(STAGES):
                if n == 0:
                    dve.wait_ge(x_in, 16)
                layer_norm(n)
                weights(n)
                dve.wait_ge(bias_added, 4 * n + 4)
                attention(st)
            feed_forward()

        @block.tensor
        def _(pe):
            mm = nc.tensor.matmul

            def three(dst, k_hi, k_lo, m_hi, m_lo, first=True, last=True):
                mm(dst, k_hi, m_hi, start=first, stop=False)
                mm(dst, k_hi, m_lo, start=False, stop=False)
                return mm(dst, k_lo, m_hi, start=False, stop=last)

            def weights(n):
                rows = P if n == 0 else DC
                pe.wait_ge(wts_in, 48 * (n + 1))
                pe.wait_ge(mt_made, 4)
                pe.wait_ge(consts, 3)
                if n:
                    pe.wait_ge(S["self"]["exp_done"], B * NP_ * QT)

                def bank_free(fill):
                    pe.wait_ge(w_out, count(fill - 2))

                for m in range(3):
                    r, c = (P, P) if m == 0 else (rows, rows)
                    by = (mt[:, (0, 1, 0)[m], :] if n == 0 else mt[:, 2, :] if m == 0 else ident[0:DC, 0:DC])
                    for k in range(2):
                        fill = NWG * n + 2 * m + k
                        bank_free(fill)
                        for i in range(4):
                            ins = mm(fill_view(fill, c)[:, i, :], raw[0:r, m, (4 * k + i) * P:(4 * k + i + 1) * P], by,
                                     start=True, stop=True)
                        ins.then_inc(w_ready, 1)
                pe.wait_ge(wo_in, 16 * (n + 1))
                for what in ("a", "b"):
                    for k in range(4):
                        odd, half = k // 2, k % 2
                        fill = NWG * n + (6 if what == "a" else 10) + k
                        bank_free(fill)
                        pe.wait_ge(w_out, NWG * n + 6)
                        r = slice(64 * odd, 64 * odd + 64)
                        for i in range(4):
                            c = 4 * half + i
                            if what == "a":
                                ins = mm(fill_view(fill, rows)[:, i, :], wt[r, 0, c, :], wt[r, 1, c, 0:rows],
                                         start=True, stop=True)
                            else:
                                ins = mm(fill_view(fill, D, rows)[:, i, :], wt[r, 2, c, 0:rows], wo[r, c, :],
                                         start=True, stop=True)
                        ins.then_inc(w_ready, 1)

            def layer_norm(n):
                for c in range(4):
                    pe.wait_ge(z_made, 4 * n + c + 1)
                    if c > 1:
                        pe.wait_ge(zt_copied, count(4 * n + c - 1))
                    bank = o_ps if c % 2 == 0 else m_ps
                    for i in range(4):
                        ins = nc.tensor.transpose(bank[:, i * P:(i + 1) * P], z[:, 4 * c + i, :], ident[:])
                    ins.then_inc(zt_ready, 1)

            def attention(st):
                s = S[st.name]

                def key_parts(kp, t):
                    if st is SELF:
                        c = slice(t * P, (t + 1) * P)
                        return zt_hi[:, kp, c], zt_lo[:, kp, c]
                    c = slice(t * P, t * P + st.krows[t])
                    return ct_hi[:, kp, c], ct_lo[0:DC, kp, c]

                def prep(b, kp, groups):
                    if st is SELF:
                        return
                    for n in groups:
                        if n == 0:
                            pe.wait_ge(ctx_in, (b + 1) * 32)
                        fill = b * (16 * NP_ + 4) + n
                        pe.wait_ge(s["mx_read"], count(fill - 1))
                        for t in CGROUPS[n]:
                            kr, o = st.krows[t], (t - CGROUPS[n][0]) * P
                            ins = nc.tensor.transpose(mx_ps[n % 2][0:DC, o:o + kr], craw[0:kr, t, :], ident[0:kr, 0:kr])
                        ins.then_inc(s["mx_ready"], 1)

                def queries(pr):
                    kp = pr.bs % 2
                    if pr.hp < st.ahead:
                        pe.wait_ge(s["zlo_done"], pr.b + 1)
                    pe.wait_ge(s["qlo_done"], count(pr.g))
                    if st is CROSS:
                        pe.wait_ge(s["out_read"], count(pr.g - st.ahead - 1))
                    for hh in range(PAIR):
                        dst = q_bank[st][0:st.qrows, hh * SQ:(hh + 1) * SQ]
                        h = pr.hp * PAIR + hh
                        ah, al = a_hi[:, h, 0:st.qrows], a_lo[:, h, 0:st.qrows]
                        zh, zl = zt_hi[:, kp, :], zt_lo[:, kp, :]
                        ins = three(dst, ah, al, zh, zl)
                    ins.then_inc(s["q_ready"], 1)

                def maxima(pr, groups):
                    kp, k = pr.bs % 2, pr.hp % st.nq
                    for n in groups:
                        if n == 0:
                            pe.wait_ge(s["qhi_done"], pr.g + 1)
                            if st is CROSS:
                                pe.wait_ge(s["mx_read"], mx_count(st, Pair(pr.b, 0, 0, NP_)))
                        pe.wait_ge(s["mx_read"], count(mx_count(st, pr) + n + 1 - len(mx_banks[st])))
                        if st is SELF:
                            for j in range(QT):
                                c = (QT * n + j) * P
                                ins = mm(mx_banks[st][0][:, j * SQ:(j + 1) * SQ], q_hi[:, k, c:c + P], zt_hi[:, kp, :],
                                         start=True, stop=True)
                        else:
                            c, x0, xw = n // 4 * P, MX0[n % 4], MXW[n % 4]
                            ins = mm(mx_ps[n % 2][:, 0:xw], q_hi[0:DC, k, c:c + P], ct_hi[0:DC, kp, x0:x0 + xw],
                                     start=True, stop=True)
                        ins.then_inc(s["mx_ready"], 1)

                def scores(pr, t):
                    kp, k, kr = pr.bs % 2, pr.hp % st.nq, st.krows[t]
                    if t == 0:
                        pe.wait_ge(s["mrow_in"][k], (pr.g // st.nq + 1) * 64)
                        pe.wait_ge(s["qlo_done"], pr.g + 1)
                    d = st.back(pr.hp, t)
                    if d <= NSB:
                        pe.wait_ge(s["exp_done"], count(pr.g * st.nt + t - d + 1))
                    dst = s_ps[st.bank(pr.hp, t)][0:kr, :]
                    kh, kl = key_parts(kp, t)
                    r = st.drows
                    mm(dst, kh, q_hi[0:r, k, :], start=True, stop=False)
                    mm(dst, kh[0:st.qrows], q_lo[0:st.qrows, k, :], start=False, stop=False)
                    mm(dst, kl, q_hi[0:st.qrows, k, :], start=False, stop=True).then_inc(s["scores_ready"], 1)

                def values(pr, t):
                    kp, k, kr = pr.bs % 2, st.slot(pr.hp, t), st.krows[t]
                    if t == 0:
                        pe.wait_ge(s["u_copied"], count(pr.g))
                        if st is CROSS and pr.hp == 0:
                            pe.wait_ge(s["vlo_done"], 2 * pr.b + 2)
                    pe.wait_ge(s["plo_done"], pr.g * st.nt + t + 1)
                    if st is SELF:
                        vh, vl = zn_hi[:, kp, t, :], zn_lo[:, kp, t, :]
                    else:
                        vh, vl = cn_hi[0:kr, kp, t, 0:DC + 1], cn_lo[0:kr, kp, t, 0:DC + 1]
                    three(u_ps[0:st.drows, :], vh, vl, p_hi[0:kr, k, :], p_lo[0:kr, k, :],
                          t == 0, t == st.nt - 1).then_inc(s["pv_done"], 1)

                def outputs(g, hp, n_queries):
                    pe.wait_ge(s["u_copied"], g + 1)
                    pe.wait_ge(s["out_read"], count(g))
                    if st is CROSS:
                        pe.wait_ge(s["qlo_done"], n_queries)
                    for hh, bank in enumerate((o_ps, m_ps)):
                        h = hp * PAIR + hh
                        for j in range(QT):
                            c = hh * SQ + j * P
                            ins = mm(bank[:, j * (D + 2):(j + 1) * (D + 2)], u_sb[0:st.drows, hp % 2, c:c + P], bm[0:st.drows, h, :],
                                     start=True, stop=True)
                    ins.then_inc(s["out_ready"], 1)

                def body(pr, last):
                    steps, nxt = plan(st, pr, last)
                    for t in range(st.nt):
                        ahead = tile_ahead(st, pr, t, LEAD_PE, last)
                        if ahead:
                            scores(*ahead)
                        after = []
                        for what, arg in steps[t]:
                            if what == "prep":
                                prep(pr.b + 1, (pr.bs + 1) % 2, arg)
                            if what == "q":
                                queries(nxt)
                            if what == "mx":
                                maxima(*arg)
                            if what == "out" and not (isinstance(pr.g, int) and pr.g == 0):
                                args = (pr.g - 1, (pr.hp - 1) % NP_, nxt.g + 1 if nxt else B * NP_)
                                if st is SELF:
                                    after = [args]
                                else:
                                    outputs(*args)
                        values(pr, t)
                        for g, hp, n_queries in after:
                            outputs(g, hp, n_queries)

                prep(0, 0, range(4))
                for pr in ahead_pairs(st):
                    queries(pr)
                    if st is SELF and pr.hp == st.ahead - 1:
                        maxima(pr, range(1))
                    else:
                        maxima(pr, range(st.mx_groups))
                for pr, t in first_tiles(st, LEAD_PE):
                    scores(pr, t)
                pairs(pe, st, body)
                outputs(B * NP_ - 1, NP_ - 1, B * NP_)

            for n, st in enumerate(STAGES):
                if n:
                    pe.wait_ge(S["self"]["out_read"], B * NP_)
                weights(n)
                layer_norm(n)
                pe.wait_ge(zt_copied, 4 * n + 4)
                pe.wait_ge(w_out, NWG * (n + 1))
                attention(st)

            pe.wait_ge(ff_in, 32)
            pe.wait_ge(S["cross"]["exp_done"], B * NP_ * CT)
            for k in range(2):
                mm(fill_bank(2 * NWG + k)[:], mt[:, 3, :], raw[:, 0, k * 512:(k + 1) * 512],
                   start=True, stop=True).then_inc(w_ready, 1)
            pe.wait_ge(S["cross"]["out_read"], B * NP_)
            layer_norm(2)
            pe.wait_ge(w_out, 2 * NWG + 2)

            def second(c):
                pe.wait_ge(act_done, FC * (c + 1))
                pe.wait_ge(ff_added, count(c - 1))
                for j in range(4):
                    for f in range(FC):
                        ins = mm(ff2_ps[c % 2][:, j * D:(j + 1) * D], ffx(c)[:, f * 512 + j * P:f * 512 + (j + 1) * P],
                                 w2[:, f, :], start=f == 0, stop=f == FC - 1)
                ins.then_inc(ff2_ready, 1)

            for c in range(4):
                pe.wait_ge(ffz_lo, c + 1)
                for f in range(FC):
                    pe.wait_ge(act_done, count(FC * c + f - 1))
                    for bank, col in ((gate_ps[f % 2], (FC + f) * P), (lin_ps[f % 2], f * P)):
                        three(bank[:], w1_hi[:, col:col + P], w1_lo[:, col:col + P], q_hi[:, c % 2, :],
                              q_lo[:, c % 2, :]).then_inc(ff1_ready, 1)
                if c:
                    second(c - 1)
            second(3)


_NAMES = ("wq1", "wk1", "wv1", "wo1", "bo1", "g1", "b1", "wq2", "wk2", "wv2", "wo2", "bo2", "g2", "b2",
          "w_ff1", "b_ff1", "w_ff2", "b_ff2", "g3", "b3")


def kernel(**inputs):
    import numpy as np
    import concourse.bacc as bacc
    from concourse.bass_utils import run_bass_kernel_spmd

    nc = bacc.Bacc("TRN2", target_bir_lowering=False, num_devices=1)
    arrays, aps = {}, {}
    for name in ("x", "ctx_768") + tuple(f"L0_xattn_{n}" for n in _NAMES):
        a = np.ascontiguousarray(inputs[name])
        arrays[f"in_{name}"] = a
        aps[name] = nc.dram_tensor(f"in_{name}", a.shape, mybir.dt.from_np(a.dtype), kind="ExternalInput").ap()
    out = nc.dram_tensor("out", inputs["x"].shape, F32, kind="ExternalOutput").ap()
    build(nc, aps["x"], aps["ctx_768"], {n: aps[f"L0_xattn_{n}"] for n in _NAMES}, out)
    r = run_bass_kernel_spmd(nc, [arrays], core_ids=[0])
    return r.results[0]["out"]
```

```python
from contextlib import ExitStack

import concourse.bass as bass
from concourse import mybir

F32 = mybir.dt.float32
F32R = mybir.dt.float32r
ACT = mybir.ActivationFunctionType
ALU = mybir.AluOpType
AX = mybir.AxisListType

P = 128
AUG = 96
EPS = 1e-5
PAIR = 2
NSB = 3
NPS = 4
LEAD_PE = 3
LEAD_ACT = 2
LEAD_DVE = 1


class Shapes:
    def __init__(self, x, ctx, wq, wff1):
        self.B, self.SQ, self.D = x.shape
        _, self.SK, self.DC = ctx.shape
        self.HD = wq.shape[1]
        self.DH = 64
        self.H = self.HD // self.DH
        self.NP = self.H // PAIR
        self.QT = self.SQ // P
        self.W = PAIR * self.SQ
        self.NSLAB = self.B * self.QT
        self.HC = self.HD // P
        self.FF = wff1.shape[1] // 2
        self.FC = self.FF // P
        self.CT = -(-self.SK // P)
        self.CLAST = self.SK - (self.CT - 1) * P
        assert self.D == P and self.DC == AUG and self.W == 512 and self.SQ == 256
        assert self.NP == 8 and self.B == 8 and self.CLAST > 64 and self.CT % 2


def count(value):
    return max(value, 0) if isinstance(value, int) else value


class Stage:

    def __init__(self, name, nt, krows, drows, qrows, ahead, nq, mx_groups, mx_per_batch, ring):
        self.name = name
        self.nt = nt
        self.krows = krows
        self.drows = drows
        self.qrows = qrows
        self.ahead = ahead
        self.nq = nq
        self.mx_groups = mx_groups
        self.mx_per_batch = mx_per_batch
        self.ring = ring

    def bank(self, hp, t):
        return self.ring[(hp * self.nt + t) % len(self.ring)]

    def slot(self, hp, t):
        return (hp * self.nt + t) % NPS

    def back(self, hp, t):
        n, i = len(self.ring), hp * self.nt + t
        return next(k for k in range(1, n + 1) if self.ring[(i - k) % n] == self.ring[i % n])


class Pair:

    def __init__(self, b, bs, hp, np_):
        self.b, self.bs, self.hp, self.np_ = b, bs, hp, np_
        self.g = b * np_ + hp

    def next(self, n, last_b):
        if self.hp + n < self.np_:
            return Pair(self.b, self.bs, self.hp + n, self.np_)
        if last_b:
            return None
        return Pair(self.b + 1, self.bs + 1, self.hp + n - self.np_, self.np_)


def build(nc, x, ctx, w, out):
    sh = Shapes(x, ctx, w["wq1"], w["w_ff1"])
    B, SQ, D, H, NP_, QT, W, CT, DC = sh.B, sh.SQ, sh.D, sh.H, sh.NP, sh.QT, sh.W, sh.CT, sh.DC
    NSLAB, HC, FC, HD = sh.NSLAB, sh.HC, sh.FC, sh.HD
    SCALE = float(sh.DH) ** -0.5
    SKP = CT * P
    MXW = [402, 400, 400, 400]
    MX0 = [0, 402, 802, 1202]
    assert MX0[-1] + MXW[-1] == sh.SK + sh.SK % 2

    SELF = Stage("self", QT, [P] * QT, P, P, 4, 4, 2, 0, [0, 1, 2, 0, 1, 2, 0, 1])
    CROSS = Stage("cross", CT, [P] * (CT - 1) + [sh.CLAST], DC + 1, DC, 2, 4, 16, 4,
                  [t % NSB for t in range(CT)] + [(t + 1) % NSB for t in range(CT)])
    STAGES = (SELF, CROSS)

    with ExitStack() as stack:
        stack.enter_context(nc.allow_non_contiguous_dma(reason="columns of at most 512 values"))

        def sb(name, shape, dt=F32):
            return stack.enter_context(nc.sbuf_tensor(name, shape, dt))

        def sem(name):
            return stack.enter_context(nc.semaphore(name))

        xs = sb("xs", [P, NSLAB, D])
        z = sb("z", [P, 2, 4, D])
        stats = sb("stats", [P, 2, 4, 6])
        mv = sb("mv", [P, 2, 4, 2])
        veps = sb("veps", [P, 2, 4])
        rstd = sb("rstd", [P, 2, 4])
        mhalf = sb("mhalf", [P, 4])
        zeros = sb("zeros", [P, CT, 1])
        ident = sb("ident", [P, P])
        fold = sb("fold", [P, P])
        gcol = sb("gcol", [P, 3])
        bcol = sb("bcol", [P, 3])
        mt = sb("mt", [P, 4, P])
        bo = sb("bo", [P, 3, D])
        bff1 = sb("bff1", [P, 2 * FC])
        raw = sb("raw", [P, 3, HD])
        wo = sb("wo", [P, HC, D])
        wt = sb("wt", [P, 3, HC, P])
        a_hi = sb("a_hi", [P, H, P], F32R)
        a_lo = sb("a_lo", [P, H, P], F32R)
        bm = sb("bm", [P, H, D + 2])
        zt_hi = sb("zt_hi", [P, 2, SQ], F32R)
        zt_lo = sb("zt_lo", [P, 2, SQ], F32R)
        zn_hi = sb("zn_hi", [P, 2, QT, P], F32R)
        zn_lo = sb("zn_lo", [P, 2, QT, P], F32R)
        craw = sb("craw", [P, CT, DC])
        ct_hi = sb("ct_hi", [DC + 1, 2, SKP], F32R)
        ct_lo = sb("ct_lo", [DC + 1, 2, SKP], F32R)
        cn_hi = sb("cn_hi", [P, 2, CT, DC + 2], F32R)
        cn_lo = sb("cn_lo", [P, 2, CT, DC + 2], F32R)
        q_hi = sb("q_hi", [P, 4, W], F32R)
        q_lo = sb("q_lo", [P, 4, W], F32R)
        p_32 = sb("p_32", [P, NPS, W])
        p_hi = sb("p_hi", [P, NPS, W], F32R)
        p_lo = sb("p_lo", [P, NPS, W], F32R)
        mxp = sb("mxp", [P, 4, 4, 4])
        negm = sb("negm", [P, 4, 4], F32R)
        u_sb = sb("u_sb", [P, 2, W])
        rden = sb("rden", [P, 4])
        o_sum = sb("o_sum", [P, QT, D])
        o_sb = sb("o_sb", [P, PAIR, QT, D])
        w1_hi = sb("w1_hi", [P, 2 * sh.FF], F32R)
        w1_lo = sb("w1_lo", [P, 2 * sh.FF], F32R)
        w2 = sb("w2", [P, FC, D])

        banks = [stack.enter_context(nc.psum_tensor(f"bank{i}", [P, 512], F32)) for i in range(8)]
        s_ps = banks[0:3]
        u_ps = banks[3]
        mx_ps = banks[4:6]
        o_ps = banks[6]
        m_ps = banks[7]
        mx_banks = {SELF: mx_ps[0:1], CROSS: mx_ps}
        FIRST_MX = {SELF: (mx_ps[0], m_ps), CROSS: (mx_ps[0], mx_ps[1], o_ps, u_ps)}
        q_bank = {SELF: mx_ps[1], CROSS: m_ps}

        gb_in = [sem(f"gb{i}_in") for i in (1, 2, 3)]
        x_in, x0_in, bias_in, consts, ctx_in, stored = (
            sem(n) for n in ("x_in", "x0_in", "bias_in", "consts", "ctx_in", "stored"))
        w_in = [sem(f"w{c}_in") for c in "qkv"]
        wo_in, ff_in, mt_made, mt_step, bias_added = (
            sem(n) for n in ("wo_in", "ff_in", "mt_made", "mt_step", "bias_added"))
        w_ready, w_hi, w_act, w_dve, bm_set, ones_set = (
            sem(n) for n in ("w_ready", "w_hi", "w_act", "w_dve", "bm_set", "ones_set"))
        wff_ready, wff_hi, wff_lo = sem("wff_ready"), sem("wff_hi"), sem("wff_lo")
        LN = ("var_ready", "rstd_made", "stat_step", "row_step", "z_made", "zt_ready")
        S = {}
        for st in STAGES:
            S[st.name] = {n: sem(f"{st.name}_{n}") for n in (
                "scores_ready", "exp_done", "plo_done", "pv_done", "q_ready", "qhi_done", "qlo_done",
                "mx_ready", "mx_read", "quarter_ready", "negm_ready", "u_copied", "out_ready", "rden_made",
                "out_read", "half_added", "pair_added", "batch_added", "zhi_done", "zlo_done", "chi_done", "vhi_done",
                "vlo_done") + LN}
        for st in STAGES:
            S[st.name]["mrow_in"] = [sem(f"{st.name}_mrow_in{k}") for k in range(st.nq)]
        FFN = {n: sem(f"ff_{n}") for n in LN}
        ff1_ready, gelu_done, act_done, ff2_ready, ff_added = (
            sem(n) for n in ("ff1_ready", "gelu_done", "act_done", "ff2_ready", "ff_added"))
        ffz_hi, ffz_lo = sem("ffz_hi"), sem("ffz_lo")

        def pairs(eng, st, body):
            def batch(b, bs, last):
                for hp in range(NP_):
                    body(Pair(b, bs, hp, NP_), last)

            batch(0, 0, False)
            with eng.Fori(0, (B - 2) // 2) as i:
                for k in range(2):
                    batch(i * 2 + (1 + k), 1 + k, False)
            batch(B - 1, B - 1, True)

        def ahead_pairs(st):
            return [Pair(0, 0, n, NP_) for n in range(st.ahead)]

        def tile_ahead(st, pr, t, n, last):
            nxt = pr.next((t + n) // st.nt, last)
            return (nxt, (t + n) % st.nt) if nxt else None

        def first_tiles(st, n):
            return [(Pair(0, 0, i // st.nt, NP_), i % st.nt) for i in range(n)]

        def needs_prep(st, pr, last):
            return not last and pr.hp + st.ahead + 1 == NP_

        def mx_count(st, pr):
            return pr.g * st.mx_groups + (pr.b + 1) * st.mx_per_batch

        def start(st):
            p = [Pair(0, 0, n, NP_) for n in range(4)]
            if st is SELF:
                return [("q", p[0]), ("b", 0), ("q", p[1]), ("mx", (p[0], range(2))), ("b", 1), ("q", p[2]),
                        ("mx", (p[1], range(2))), ("b", 2), ("q", p[3]), ("mx", (p[2], range(2))), ("b", 3),
                        ("mx", (p[3], range(1)))]
            steps = [("q", p[0])]
            for k in range(4):
                steps += [("b", k), ("mx", (p[0], share(k, 4)))]
            return steps + [("q", p[1])]

        def share(k, n):
            return range(16 * k // n, 16 * (k + 1) // n)

        def plan(st, pr, last):
            steps = [[] for _ in range(st.nt)]
            nxt = pr.next(st.ahead, last)
            prep = needs_prep(st, pr, last)
            if st is SELF:
                before = pr.next(st.ahead - 1, last)
                if before:
                    steps[0].append(("mx", (before, range(1, 2))))
                if nxt:
                    steps[0].append(("q", None))
                steps[0].append(("scale", 2))
                if nxt:
                    steps[1].append(("mx", (nxt, range(0, 1))))
                if prep:
                    steps[1].append(("z", None))
                steps[1].append(("out", None))
                return steps, nxt
            first = isinstance(pr.g, int) and pr.g == 0
            n0, n1 = (7, CT) if first else (1, 9) if prep else (1, CT)
            if first:
                for k in range(6):
                    steps[k].append(("mx", (pr.next(1, last), share(k, 6))))
            if nxt:
                steps[n0 - 1].append(("q", None))
                for k in range(n0, n1):
                    steps[k].append(("mx", (nxt, share(k - n0, n1 - n0))))
            steps[2].append(("out", None))
            steps[3].append(("scale", 1))
            if prep:
                steps[4].append(("z", None))
                for k in range(4):
                    steps[9 + k].append(("prep", range(k, k + 1)))
            return steps, nxt

        CGROUPS = [range(0, 4), range(4, 8), range(8, 12), range(12, CT)]
        NWG = 14
        ACT_FILLS = (1, 3, 5, 11, 13)
        CTX_AFTER = {1: 0, 3: 1, 5: 2, 7: 3}
        LAST_AFTER, SUM_AFTER, Z_AFTER = 1, 5, 7

        def by_act(fill):
            return fill % NWG in ACT_FILLS

        def act_count(fill):
            return sum(by_act(i) for i in range(fill + 1))

        def dve_count(fill):
            return fill + 1 - act_count(fill)

        def width(n):
            return (len(CGROUPS[n]) - 1) * P + (sh.CLAST if n == len(CGROUPS) - 1 else P)

        def heads(t, half, odd, c):
            return t[:, 8 * half + odd:8 * half + odd + 7:2, 0:c]

        def fill_bank(fill):
            return s_ps[fill % NSB]

        def fill_view(fill, c, rows=P):
            return fill_bank(fill)[0:rows, 0:4 * c].rearrange("p (h c) -> p h c", h=4)

        t_ps = [s_ps[2], u_ps, o_ps, m_ps]
        gate_ps = [s_ps[0], mx_ps[0]]
        lin_ps = [s_ps[1], mx_ps[1]]
        ff2_ps = [s_ps[2], u_ps]

        def ffx(c):
            t = wt[:, 0:2].rearrange("p a c d -> p (a c d)") if c % 2 == 0 else raw[:, 1:3].rearrange("p a c -> p (a c)")
            return t

        block = stack.enter_context(nc.Block())

        def load_context(sp, b):
            full = (CT - 1) * P
            one = isinstance(b, int)
            src = ctx[b] if one else ctx[bass.ds(b, 1)].rearrange("o s d -> (o s) d")
            sp.dma_start(craw[:, 0:CT - 1, :], src[0:full, :].rearrange("(t p) d -> p t d", p=P)).then_inc(ctx_in, 16)
            sp.dma_start(craw[0:sh.CLAST, CT - 1, :], src[full:sh.SK, :]).then_inc(ctx_in, 16)

        def mrows(sp, st):
            s = S[st.name]

            def row(pr):
                if st is SELF:
                    sp.wait_ge(s["mx_read"], mx_count(st, pr) + st.mx_groups)
                elif not (isinstance(pr.g, int) and pr.g == 0):
                    sp.wait_ge(s["negm_ready"], pr.g)
                q = pr.hp % st.nq
                for j in range(4):
                    if st is CROSS and isinstance(pr.g, int) and pr.g == 0:
                        sp.wait_ge(s["quarter_ready"], j + 1)
                    sp.dma_start(q_hi[AUG:AUG + 1, q, j * P:(j + 1) * P].bitcast(F32),
                                 negm[:, q, j:j + 1].bitcast(F32)).then_inc(s["mrow_in"][q], 16)

            def body(pr, last):
                if st is CROSS and pr.hp == 0 and not last:
                    sp.wait_ge(s["vlo_done"], 2 * pr.b + 2)
                    sp.wait_ge(s["mx_ready"], (pr.b + 1) * 4 + pr.b * 128)
                    load_context(sp, pr.b + 1)
                nxt = pr.next(st.ahead, last)
                if nxt:
                    row(nxt)

            for pr in ahead_pairs(st):
                row(pr)
            if st is SELF:
                sp.wait_ge(w_ready, NWG)
                sp.dma_start(wo[:], w["wo2"].rearrange("(c p) d -> p c d", p=P)).then_inc(wo_in, 16)
            else:
                sp.wait_ge(w_ready, NWG + 6)
                sp.dma_start(raw[:, 0, :], w["w_ff1"]).then_inc(ff_in, 16)
                sp.dma_start(w2[:], w["w_ff2"].rearrange("(c p) d -> p c d", p=P)).then_inc(ff_in, 16)
            pairs(sp, st, body)

        @block.sync
        def _(sp):
            for i, n in enumerate(("wq1", "wk1", "wv1")):
                sp.dma_start(raw[:, i, :], w[n]).then_inc(w_in[i], 16)
            sp.dma_start(wo[:], w["wo1"].rearrange("(c p) d -> p c d", p=P)).then_inc(wo_in, 16)
            sp.dma_start(xs[:, QT:], x[1:B].rearrange("b (t p) d -> p (b t) d", p=P)).then_inc(x_in, 16)
            load_context(sp, 0)
            sp.wait_ge(w_ready, 6)
            for i, n in enumerate(("wq2", "wk2", "wv2")):
                sp.dma_start(raw[0:w[n].shape[0], i, :], w[n]).then_inc(w_in[i], 16)
            mrows(sp, SELF)
            mrows(sp, CROSS)
            for c in range(4):
                sp.wait_ge(ff_added, c + 1)
                sp.dma_start(out.rearrange("b (t p) d -> p (b t) d", p=P)[:, 4 * c:4 * c + 4, :],
                             xs[:, 4 * c:4 * c + 4, :]).then_inc(stored, 16)
            sp.wait_ge(stored, 4 * 16)

        def split_context(pool, b, kp):
            s = S["cross"]
            pool.wait_ge(ctx_in, (b + 1) * 32)
            for n, (hi, t0, t1) in enumerate(((P, 0, CT - 1), (sh.CLAST, CT - 1, CT))):
                pool.wait_ge(s["vlo_done"], 2 * b + n)
                nc.gpsimd.tensor_tensor(out=cn_hi[0:hi, kp, t0:t1, 0:DC], in0=craw[0:hi, t0:t1, :],
                                        in1=zeros[0:hi, 0:t1 - t0, 0:1].to_broadcast([hi, t1 - t0, DC]),
                                        op=ALU.add).then_inc(s["vhi_done"], 1)
                pool.wait_ge(s["vhi_done"], 2 * b + n + 1)
                nc.gpsimd.tensor_tensor(out=cn_lo[0:hi, kp, t0:t1, 0:DC], in0=craw[0:hi, t0:t1, :],
                                        in1=cn_hi[0:hi, kp, t0:t1, 0:DC].bitcast(F32),
                                        op=ALU.subtract).then_inc(s["vlo_done"], 1)

        @block.gpsimd
        def _(pool):
            g = nc.gpsimd

            def power(s, c, k, n):
                pool.wait_ge(s["var_ready"], c + 1)
                g.tensor_tensor(out=rstd[:, k, 0:n], in0=veps[:, k, 0:n], in1=mhalf[:, 0:n],
                                op=ALU.pow).then_inc(s["rstd_made"], 1)

            def add_pairs(st):
                s = S[st.name]
                if st is CROSS:
                    split_context(pool, 0, 0)

                def body(pr, last):
                    if st is CROSS and needs_prep(st, pr, last):
                        if not (isinstance(pr.b, int) and pr.b == 0):
                            pool.wait_ge(s["pv_done"], pr.b * (NP_ * CT))
                        split_context(pool, pr.b + 1, (pr.bs + 1) % 2)
                    if not last and pr.hp == 0:
                        power(s, pr.b + 1, (pr.bs + 1) % 2, QT)
                    if last and st is SELF and pr.hp == 5:
                        power(S["cross"], 0, 0, QT)
                    if last and st is CROSS and pr.hp == NP_ - 1:
                        for c in range(3):
                            power(FFN, c, c % 2, 4)
                    pool.wait_ge(s["out_read"], pr.g + 1)
                    if pr.hp == 0:
                        if not (isinstance(pr.b, int) and pr.b == 0):
                            pool.wait_ge(s["batch_added"], pr.b)
                        n = STAGES.index(st)
                        before = bo[:, n:n + 1, :].to_broadcast([P, QT, D])
                    else:
                        pool.wait_ge(s["pair_added"], pr.g)
                        before = o_sum[:]
                    g.tensor_tensor(out=o_sum[:], in0=o_sb[:, 0], in1=before, op=ALU.add).then_inc(s["half_added"], 1)
                    pool.wait_ge(s["half_added"], pr.g + 1)
                    g.tensor_tensor(out=o_sum[:], in0=o_sb[:, 1], in1=o_sum[:], op=ALU.add).then_inc(s["pair_added"], 1)

                pairs(pool, st, body)

            g.memset(ident[:], 0.0).then_inc(consts, 1)
            pool.wait_ge(consts, 1)
            g.affine_select(out=ident[:], in_=ident[:], compare_op=ALU.not_equal, fill=1.0, base=0,
                            pattern=[[-1, P]], channel_multiplier=1).then_inc(consts, 1)
            pool.wait_ge(consts, 2)
            g.affine_select(out=fold[:], in_=ident[:], compare_op=ALU.not_equal, fill=-1.0, base=-AUG,
                            pattern=[[0, P]], channel_multiplier=1).then_inc(consts, 1)
            g.memset(mhalf[:], -0.5).then_inc(consts, 1)
            g.memset(zeros[:], 0.0).then_inc(consts, 1)
            g.memset(bm[:], 0.0).then_inc(bm_set, 1)
            pool.wait_ge(bm_set, 1)
            g.memset(bm[AUG:AUG + 1, :, D:D + 1], 1.0).then_inc(bm_set, 1)
            g.memset(ct_hi[AUG:AUG + 1].bitcast(F32), 1.0).then_inc(ones_set, 1)
            pool.wait_ge(ones_set, 1)
            g.memset(cn_hi[:, :, :, DC:DC + 2].bitcast(F32), 1.0).then_inc(ones_set, 1)
            g.memset(cn_lo[:, :, :, DC:DC + 2].bitcast(F32), 0.0).then_inc(ones_set, 1)
            pool.wait_ge(consts, 5)
            power(S["self"], 0, 0, QT)
            pool.wait_ge(bias_in, 64)
            add_pairs(SELF)
            pool.wait_ge(S["self"]["pair_added"], B * NP_)
            g.memset(bm[AUG:AUG + 1, :, 0:D], 0.0).then_inc(bm_set, 1)
            pool.wait_ge(bm_set, 3)
            add_pairs(CROSS)
            for c in range(4):
                if c == 0:
                    power(FFN, 3, 1, 4)
                pool.wait_ge(FFN["z_made"], c + 1)
                v = xs[:, 4 * c:4 * c + 4, :]
                g.tensor_tensor(out=v, in0=v, in1=bo[:, 2:3, :].to_broadcast([P, 4, D]),
                                op=ALU.add).then_inc(bias_added, 1)

        @block.scalar
        def _(act):
            def copy(dst, src):
                return nc.scalar.activation(dst, src, ACT.Copy)

            def context_groups(groups, b, kp):
                s = S["cross"]
                for n in groups:
                    fill = b * (16 * NP_ + 4) + n
                    act.wait_ge(s["mx_ready"], fill + 1)
                    cols = slice(CGROUPS[n][0] * P, CGROUPS[n][0] * P + width(n))
                    copy(ct_hi[0:DC, kp, cols], mx_ps[n % 2][0:DC, 0:width(n)]).then_inc(s["chi_done"], 1)

            def b_product(n, k):
                fill, rows = NWG * n + 10 + k, P if n == 0 else DC
                if by_act(fill):
                    act.wait_ge(w_ready, fill + 1)
                    act.wait_ge(bm_set, 2 + n)
                    copy(heads(bm, k % 2, k // 2, D)[0:rows], fill_view(fill, D, rows)).then_inc(w_act, 1)

            def weights(n, after):
                rows = P if n == 0 else DC
                for i in range(NWG - 4):
                    fill = NWG * n + i
                    if by_act(fill) or 6 <= i < 10:
                        act.wait_ge(w_ready, fill + 1)
                    if i < 6 and by_act(fill):
                        m, k = i // 2, i % 2
                        c = P if m == 0 else rows
                        copy(wt[:, m, 4 * k:4 * k + 4, 0:c], fill_view(fill, c)).then_inc(w_act, 1)
                    if 6 <= i < 10:
                        odd, half = (i - 6) // 2, (i - 6) % 2
                        copy(heads(a_hi, half, odd, rows), fill_view(fill, rows)).then_inc(w_hi, 1)
                    if n and i in CTX_AFTER:
                        context_groups([CTX_AFTER[i]], 0, 0)
                    for step in after.get(i, ()):
                        step()

            def scale_out(s, g):
                act.wait_ge(s["rden_made"], g + 1)
                act.wait_ge(s["pair_added"], count(g))
                for hh, bank in enumerate((o_ps, m_ps)):
                    for j in range(QT):
                        i = nc.scalar.activation(o_sb[:, hh, j, :], bank[:, j * (D + 2):j * (D + 2) + D], ACT.Copy,
                                                 scale=rden[:, QT * hh + j:QT * hh + j + 1])
                i.then_inc(s["out_read"], 1)

            def z_parts(st, b, kp):
                s = S[st.name]
                act.wait_ge(s["zt_ready"], b + 1)
                i = copy(zt_hi[:, kp, :], q_bank[st][:, 0:SQ])
                if st is SELF:
                    i = copy(zn_hi[:, kp, :, :], z[:, kp, 0:QT, :])
                i.then_inc(s["zhi_done"], 1)

            def attention(st):
                s = S[st.name]

                def queries(pr):
                    act.wait_ge(s["q_ready"], pr.g + 1)
                    copy(q_hi[0:st.qrows, pr.hp % st.nq, :], q_bank[st][0:st.qrows, :]).then_inc(s["qhi_done"], 1)

                def u_copy(g, k):
                    act.wait_ge(s["pv_done"], (g + 1) * st.nt)
                    act.wait_ge(s["out_ready"], count(g - 1))
                    copy(u_sb[0:st.drows, k, :], u_ps[0:st.drows, :]).then_inc(s["u_copied"], 1)

                def exponentials(pr, t):
                    r, bank, k, kr = pr.g * st.nt + t, st.bank(pr.hp, t), st.slot(pr.hp, t), st.krows[t]
                    act.wait_ge(s["scores_ready"], r + 1)
                    act.wait_ge(s["pv_done"], count(r - NPS + 1))
                    nc.scalar.activation(p_32[0:kr, k, :], s_ps[bank][0:kr, :], ACT.Exp, scale=SCALE)
                    nc.scalar.activation(p_hi[0:kr, k, :], s_ps[bank][0:kr, :], ACT.Exp,
                                         scale=SCALE).then_inc(s["exp_done"], 1)

                def body(pr, last):
                    steps, nxt = plan(st, pr, last)
                    for t in range(st.nt):
                        if t == 0 and not (isinstance(pr.g, int) and pr.g == 0):
                            u_copy(pr.g - 1, (pr.hp - 1) % 2)
                        ahead = tile_ahead(st, pr, t, LEAD_ACT, last)
                        if ahead:
                            exponentials(*ahead)
                        for what, arg in steps[t]:
                            if what == "z":
                                z_parts(st, pr.b + 1, (pr.bs + 1) % 2)
                            if what == "prep":
                                context_groups(arg, pr.b + 1, (pr.bs + 1) % 2)
                            if what == "q":
                                queries(nxt)
                            if what == "scale" and not (isinstance(pr.g, int) and pr.g < arg):
                                scale_out(s, pr.g - arg)

                for what, arg in start(st):
                    if what == "q":
                        queries(arg)
                    if what == "b":
                        b_product(STAGES.index(st), arg)
                for pr, t in first_tiles(st, LEAD_ACT):
                    exponentials(pr, t)
                pairs(act, st, body)
                if st is SELF:
                    scale_out(s, B * NP_ - 2)
                u_copy(B * NP_ - 1, (NP_ - 1) % 2)

            for i in (1, 2, 3):
                act.dma_start(gcol[:, i - 1:i], w[f"g{i}"].rearrange("(p o) -> p o", o=1)).then_inc(gb_in[i - 1], 16)
                act.dma_start(bcol[:, i - 1:i], w[f"b{i}"].rearrange("(p o) -> p o", o=1)).then_inc(gb_in[i - 1], 16)
                if i == 1:
                    act.dma_start(xs[:, 0:QT], x[0].rearrange("(t p) d -> p t d", p=P)).then_inc(x0_in, 16)
            for i, n in enumerate(("bo1", "bo2", "b_ff2")):
                act.dma_start(bo[:, i, :], w[n].rearrange("(o d) -> o d", o=1).to_broadcast([P, D])).then_inc(bias_in, 16)
            act.dma_start(bff1[:], w["b_ff1"].rearrange("(c p) -> p c", p=P)).then_inc(bias_in, 16)
            def z_first(st):
                return [lambda: z_parts(st, 0, 0)]

            weights(0, {Z_AFTER: z_first(SELF)})
            attention(SELF)
            weights(1, {LAST_AFTER: [lambda: scale_out(S["self"], B * NP_ - 1)], Z_AFTER: z_first(CROSS)})
            attention(CROSS)
            for k in range(2):
                act.wait_ge(wff_ready, k + 1)
                copy(w1_hi[:, k * 512:(k + 1) * 512], s_ps[k][:]).then_inc(wff_hi, 1)

            def high(c):
                act.wait_ge(FFN["zt_ready"], c + 1)
                copy(q_hi[:, c, :], t_ps[c][:]).then_inc(ffz_hi, 1)

            high(0)
            scale_out(S["cross"], B * NP_ - 1)
            high(1)
            act.wait_ge(bias_in, 64)
            for c in range(4):
                if c >= 2:
                    high(c)
                for f in range(FC):
                    act.wait_ge(ff1_ready, 8 * c + 2 * f + 1)
                    act.wait_ge(act_done, count(FC * c + f - 1))
                    nc.scalar.activation(p_32[:, f % 2, :], gate_ps[f % 2][:], ACT.Gelu,
                                         bias=bff1[:, FC + f:FC + f + 1]).then_inc(gelu_done, 1)

        @block.vector
        def _(dve):
            v = nc.vector

            def context_groups(groups, b, kp):
                s = S["cross"]
                for n in groups:
                    dve.wait_ge(s["chi_done"], b * 4 + n + 1)
                    cols = slice(CGROUPS[n][0] * P, CGROUPS[n][0] * P + width(n))
                    i = v.tensor_tensor(out=ct_lo[0:DC, kp, cols], in0=mx_ps[n % 2][0:DC, 0:width(n)],
                                        in1=ct_hi[0:DC, kp, cols].bitcast(F32), op=ALU.subtract)
                    if n == len(CGROUPS) - 1:
                        i = v.tensor_copy(ct_hi[0:DC, kp, sh.SK:sh.SK + 1], mx_ps[n % 2][0:DC, width(n) - 1:width(n)])
                    i.then_inc(s["mx_read"], 1)

            def b_product(n, k):
                fill, rows = NWG * n + 10 + k, P if n == 0 else DC
                if not by_act(fill):
                    dve.wait_ge(bm_set, 2 + n)
                    dve.wait_ge(w_ready, fill + 1)
                    v.tensor_copy(heads(bm, k % 2, k // 2, D)[0:rows], fill_view(fill, D, rows)).then_inc(w_dve, 1)

            def weights(n, after):
                rows = P if n == 0 else DC
                for i in range(NWG - 4):
                    fill = NWG * n + i
                    if not by_act(fill):
                        if i < 6:
                            m, k = i // 2, i % 2
                            c = P if m == 0 else rows
                            dve.wait_ge(w_ready, fill + 1)
                            v.tensor_copy(wt[:, m, 4 * k:4 * k + 4, 0:c], fill_view(fill, c)).then_inc(w_dve, 1)
                        else:
                            odd, half = (i - 6) // 2, (i - 6) % 2
                            dve.wait_ge(w_hi, 4 * n + i - 6 + 1)
                            v.tensor_tensor(out=heads(a_lo, half, odd, rows), in0=fill_view(fill, rows),
                                            in1=heads(a_hi, half, odd, rows).bitcast(F32), op=ALU.subtract).then_inc(w_dve, 1)
                    if n and i in CTX_AFTER:
                        context_groups([CTX_AFTER[i]], 0, 0)
                    for step in after.get(i, ()):
                        step()

            def make_mt(parts):
                dve.wait_ge(consts, 3)
                for k, i in parts:
                    dve.wait_ge(gb_in[i], 32)
                    v.tensor_scalar(mt[:, k, :], fold[:], gcol[:, i:i + 1], None, ALU.mult).then_inc(mt_step, 1)
                for k, i in parts:
                    dve.wait_ge(mt_step, k + 1)
                    col = mt[:, k, AUG:AUG + 1]
                    if k == 1:
                        ins = v.memset(col, 0.0)
                    else:
                        ins = v.tensor_copy(col, bcol[:, i:i + 1])
                    ins.then_inc(mt_made, 1)

            def row_tiles(b):
                return [xs[:, bass.ds(b * QT + i, 1), :].rearrange("p o d -> p (o d)") for i in range(QT)]

            def ln_stats(s, tiles, c, k):
                n = len(tiles)
                for i in range(n):
                    v.bn_stats(stats[:, k, i, :], tiles[i]).then_inc(s["stat_step"], 1)
                dve.wait_ge(s["stat_step"], c * (2 * n) + n)
                v.tensor_copy(veps[:, k, 0:1], stats[:, k, 0, 0:1])
                for i in range(n):
                    v.bn_aggr(mv[:, k, i, :], stats[:, k, i, :]).then_inc(s["stat_step"], 1)
                dve.wait_ge(s["stat_step"], c * (2 * n) + 2 * n)
                v.tensor_scalar(veps[:, k, 0:n], mv[:, k, 0:n, 1], EPS, None, ALU.add).then_inc(s["var_ready"], 1)

            def ln_rows(s, tiles, c, k):
                n = len(tiles)
                dve.wait_ge(s["rstd_made"], c + 1)
                for i in range(n):
                    v.tensor_scalar(z[:, k, i, :], tiles[i], mv[:, k, i, 0:1], rstd[:, k, i:i + 1],
                                    ALU.subtract, ALU.mult).then_inc(s["row_step"], 1)
                dve.wait_ge(s["row_step"], c * n + n)
                v.memset(z[:, k, 0:n, AUG:AUG + 1], 1.0).then_inc(s["z_made"], 1)

            def z_parts(st, b, kp):
                s = S[st.name]
                dve.wait_ge(s["zhi_done"], b + 1)
                i = v.tensor_tensor(out=zt_lo[:, kp, :], in0=q_bank[st][:, 0:SQ],
                                    in1=zt_hi[:, kp, :].bitcast(F32), op=ALU.subtract)
                if st is SELF:
                    i = v.tensor_tensor(out=zn_lo[:, kp, :, :], in0=z[:, kp, 0:QT, :],
                                        in1=zn_hi[:, kp, :, :].bitcast(F32), op=ALU.subtract)
                i.then_inc(s["zlo_done"], 1)

            def denominators(st, g):
                s = S[st.name]
                dve.wait_ge(s["out_ready"], g + 1)
                for hh, bank in enumerate((o_ps, m_ps)):
                    den = bank[:, 0:QT * (D + 2)].rearrange("p (j c) -> p j c", j=QT)[:, :, D:D + 1]
                    i = v.reciprocal(rden[:, QT * hh:QT * hh + QT].rearrange("p (j o) -> p j o", o=1), den)
                i.then_inc(s["rden_made"], 1)

            def add_batch(st, b):
                s = S[st.name]
                dve.wait_ge(s["pair_added"], (b + 1) * NP_)
                rows = xs[:, bass.ds(b * QT, QT), :]
                v.tensor_tensor(out=rows, in0=o_sum[:], in1=rows, op=ALU.add).then_inc(s["batch_added"], 1)

            def next_norm(st, hp, t):
                if st is SELF and (hp, t) == (6, 1):
                    ln_stats(S["cross"], row_tiles(0), 0, 0)
                if st is CROSS and hp == NP_ - 1:
                    if t == 4:
                        ln_stats(FFN, chunk_tiles(0), 0, 0)
                    if t == 5:
                        ln_stats(FFN, chunk_tiles(1), 1, 1)
                    if t == 6:
                        ln_rows(FFN, chunk_tiles(0), 0, 0)
                    if t == 7:
                        ln_rows(FFN, chunk_tiles(1), 1, 1)
                    if t == 8:
                        ln_stats(FFN, chunk_tiles(2), 2, 0)

            def attention(st):
                s = S[st.name]

                def queries(pr):
                    k = pr.hp % st.nq
                    dve.wait_ge(s["qhi_done"], pr.g + 1)
                    v.tensor_tensor(out=q_lo[0:st.qrows, k, :], in0=q_bank[st][0:st.qrows, :],
                                    in1=q_hi[0:st.qrows, k, :].bitcast(F32), op=ALU.subtract).then_inc(s["qlo_done"], 1)

                def maxima(pr, groups, mx=mx_banks[st]):
                    k = pr.hp % st.nq
                    for n in groups:
                        dve.wait_ge(s["mx_ready"], mx_count(st, pr) + n + 1)
                        if n == 0:
                            dve.wait_ge(s["mrow_in"][k], count(pr.g // st.nq * 64))
                        if st is SELF:
                            src = mx[n % len(mx)][:].rearrange("p (j k) -> p j k", j=QT)
                            v.tensor_reduce(negm[:, k, QT * n:QT * n + QT], src, AX.X, ALU.max,
                                            negate=True).then_inc(s["mx_read"], 1)
                        else:
                            v.tensor_reduce(mxp[:, k, n // 4, n % 4:n % 4 + 1], mx[n % len(mx)][:, 0:MXW[n % 4]],
                                            AX.X, ALU.max).then_inc(s["mx_read"], 1)
                    if st is CROSS and isinstance(pr.g, int) and pr.g == 0:
                        dve.wait_ge(s["mx_read"], mx_count(st, pr) + n + 1)
                        v.tensor_reduce(negm[:, k, n // 4:n // 4 + 1], mxp[:, k, n // 4], AX.X, ALU.max,
                                        negate=True).then_inc(s["quarter_ready"], 1)
                    elif st is CROSS and n == st.mx_groups - 1:
                        dve.wait_ge(s["mx_read"], mx_count(st, pr) + n + 1)
                        v.tensor_reduce(negm[:, k, :], mxp[:, k], AX.X, ALU.max, negate=True).then_inc(s["negm_ready"], 1)

                def low_part(pr, t):
                    k, kr = st.slot(pr.hp, t), st.krows[t]
                    dve.wait_ge(s["exp_done"], pr.g * st.nt + t + 1)
                    v.tensor_tensor(out=p_lo[0:kr, k, :], in0=p_32[0:kr, k, :], in1=p_hi[0:kr, k, :].bitcast(F32),
                                    op=ALU.subtract).then_inc(s["plo_done"], 1)

                def body(pr, last):
                    steps, nxt = plan(st, pr, last)
                    for t in range(st.nt):
                        ahead = tile_ahead(st, pr, t, LEAD_DVE, last)
                        if ahead:
                            low_part(*ahead)
                        for what, arg in steps[t]:
                            if what == "z":
                                z_parts(st, pr.b + 1, (pr.bs + 1) % 2)
                            if what == "prep":
                                context_groups(arg, pr.b + 1, (pr.bs + 1) % 2)
                            if what == "q":
                                queries(nxt)
                            if what == "mx":
                                maxima(*arg)
                            if what == "out" and not (isinstance(pr.g, int) and pr.g == 0):
                                denominators(st, pr.g - 1)
                        if t == 0 and pr.hp == 2 and not (isinstance(pr.b, int) and pr.b == 0):
                            add_batch(st, pr.b - 1)
                        if t == 1 and pr.hp == 1 and not last:
                            ln_stats(s, row_tiles(pr.b + 1), pr.b + 1, (pr.bs + 1) % 2)
                        if t == 1 and pr.hp == 2 and not last:
                            ln_rows(s, row_tiles(pr.b + 1), pr.b + 1, (pr.bs + 1) % 2)
                        if last:
                            next_norm(st, pr.hp, t)

                for what, arg in start(st):
                    if what == "q":
                        queries(arg)
                    if what == "b":
                        b_product(STAGES.index(st), arg)
                    if what == "mx":
                        maxima(*arg, FIRST_MX[st])
                for pr, t in first_tiles(st, LEAD_DVE):
                    low_part(pr, t)
                pairs(dve, st, body)

            def chunk_tiles(c):
                return [xs[:, 4 * c + i, :] for i in range(4)]

            def feed_forward():
                for k in range(2):
                    dve.wait_ge(wff_hi, k + 1)
                    cols = slice(k * 512, (k + 1) * 512)
                    v.tensor_tensor(out=w1_lo[:, cols], in0=s_ps[k][:], in1=w1_hi[:, cols].bitcast(F32),
                                    op=ALU.subtract).then_inc(wff_lo, 1)
                low(0)
                denominators(CROSS, B * NP_ - 1)
                low(1)
                gated(0)
                ln_rows(FFN, chunk_tiles(2), 2, 0)
                gated(1)
                low(2)
                add_batch(CROSS, B - 1)
                dve.wait_ge(S["cross"]["batch_added"], B)
                ln_stats(FFN, chunk_tiles(3), 3, 1)
                ln_rows(FFN, chunk_tiles(3), 3, 1)
                ff_add(0)
                gated(2)
                low(3)
                ff_add(1)
                gated(3)
                ff_add(2)
                ff_add(3)

            def low(c):
                dve.wait_ge(ffz_hi, c + 1)
                v.tensor_tensor(out=q_lo[:, c, :], in0=t_ps[c][:], in1=q_hi[:, c, :].bitcast(F32),
                                op=ALU.subtract).then_inc(ffz_lo, 1)

            def gated(c):
                dve.wait_ge(ff2_ready, count(c - 1))
                for f in range(FC):
                    dve.wait_ge(gelu_done, FC * c + f + 1)
                    dve.wait_ge(ff1_ready, 2 * (FC * c + f) + 2)
                    v.scalar_tensor_tensor(out=ffx(c)[:, f * 512:(f + 1) * 512], in0=lin_ps[f % 2][:],
                                           scalar=bff1[:, f:f + 1], in1=p_32[:, f % 2, :],
                                           op0=ALU.add, op1=ALU.mult).then_inc(act_done, 1)

            def ff_add(c):
                dve.wait_ge(ff2_ready, c + 1)
                dve.wait_ge(bias_added, c + 1)
                r = xs[:, 4 * c:4 * c + 4, :]
                v.tensor_tensor(out=r, in0=ff2_ps[c % 2][:].rearrange("p (j d) -> p j d", j=4), in1=r,
                                op=ALU.add).then_inc(ff_added, 1)

            make_mt(((0, 0), (1, 0)))
            dve.wait_ge(x0_in, 16)
            ln_stats(S["self"], row_tiles(0), 0, 0)
            ln_rows(S["self"], row_tiles(0), 0, 0)
            weights(0, {Z_AFTER: [lambda: z_parts(SELF, 0, 0)]})
            make_mt(((2, 1), (3, 2)))
            dve.wait_ge(x_in, 16)
            attention(SELF)
            ln_rows(S["cross"], row_tiles(0), 0, 0)
            weights(1, {LAST_AFTER: [lambda: denominators(SELF, B * NP_ - 1)],
                        SUM_AFTER: [lambda: add_batch(SELF, B - 1)],
                        Z_AFTER: [lambda: z_parts(CROSS, 0, 0)]})
            dve.wait_ge(S["self"]["batch_added"], B)
            attention(CROSS)
            feed_forward()

        @block.tensor
        def _(pe):
            mm = nc.tensor.matmul

            def three(dst, k_hi, k_lo, m_hi, m_lo, first=True, last=True):
                mm(dst, k_hi, m_hi, start=first, stop=False)
                mm(dst, k_hi, m_lo, start=False, stop=False)
                return mm(dst, k_lo, m_hi, start=False, stop=last)

            def context_groups(groups, b, kp):
                s = S["cross"]
                for n in groups:
                    if n == 0:
                        pe.wait_ge(ctx_in, (b + 1) * 32)
                    fill = b * (16 * NP_ + 4) + n
                    pe.wait_ge(s["mx_read"], count(fill - 1))
                    for t in CGROUPS[n]:
                        kr, o = CROSS.krows[t], (t - CGROUPS[n][0]) * P
                        ins = nc.tensor.transpose(mx_ps[n % 2][0:DC, o:o + kr], craw[0:kr, t, :], ident[0:kr, 0:kr])
                    ins.then_inc(s["mx_ready"], 1)

            def bank_free(fill):
                if fill >= NSB:
                    if by_act(fill - NSB):
                        pe.wait_ge(w_act, act_count(fill - NSB))
                    else:
                        pe.wait_ge(w_dve, dve_count(fill - NSB))

            def weights(n, after):
                rows = P if n == 0 else DC
                pe.wait_ge(mt_made, 2 if n == 0 else 4)
                pe.wait_ge(consts, 3)
                if n:
                    pe.wait_ge(S["self"]["exp_done"], B * NP_ * QT)

                def others(i):
                    if n and i in CTX_AFTER:
                        context_groups([CTX_AFTER[i]], 0, 0)
                    for step in after.get(i, ()):
                        step()

                for m in range(3):
                    pe.wait_ge(w_in[m], 16 * (n + 1))
                    r, c = (P, P) if m == 0 else (rows, rows)
                    by = (mt[:, (0, 1, 0)[m], :] if n == 0 else mt[:, 2, :] if m == 0 else ident[0:DC, 0:DC])
                    for k in range(2):
                        fill = NWG * n + 2 * m + k
                        bank_free(fill)
                        for i in range(4):
                            ins = mm(fill_view(fill, c)[:, i, :], raw[0:r, m, (4 * k + i) * P:(4 * k + i + 1) * P], by,
                                     start=True, stop=True)
                        ins.then_inc(w_ready, 1)
                        others(2 * m + k)
                for k in range(4):
                    fill = NWG * n + 6 + k
                    bank_free(fill)
                    pe.wait_ge(w_act, act_count(NWG * n + 5))
                    pe.wait_ge(w_dve, dve_count(NWG * n + 5))
                    odd, half = k // 2, k % 2
                    r = slice(64 * odd, 64 * odd + 64)
                    for i in range(4):
                        c = 4 * half + i
                        ins = mm(fill_view(fill, rows)[:, i, :], wt[r, 0, c, :], wt[r, 1, c, 0:rows],
                                 start=True, stop=True)
                    ins.then_inc(w_ready, 1)
                    others(6 + k)

            def b_product(n, k):
                fill, rows = NWG * n + 10 + k, P if n == 0 else DC
                if k == 0:
                    pe.wait_ge(wo_in, 16 * (n + 1))
                bank_free(fill)
                odd, half = k // 2, k % 2
                r = slice(64 * odd, 64 * odd + 64)
                for i in range(4):
                    c = 4 * half + i
                    ins = mm(fill_view(fill, D, rows)[:, i, :], wt[r, 2, c, 0:rows], wo[r, c, :],
                             start=True, stop=True)
                ins.then_inc(w_ready, 1)

            def z_transposed(st, b, kp, n_queries, n_out):
                s = S[st.name]
                pe.wait_ge(s["z_made"], b + 1)
                pe.wait_ge(s["qlo_done"], n_queries)
                if st is CROSS:
                    pe.wait_ge(s["out_read"], n_out)
                for j in range(QT):
                    ins = nc.tensor.transpose(q_bank[st][:, j * P:(j + 1) * P], z[:, kp, j, :], ident[:])
                ins.then_inc(s["zt_ready"], 1)

            def outputs(st, g, hp, n_queries):
                s = S[st.name]
                pe.wait_ge(s["u_copied"], g + 1)
                pe.wait_ge(s["out_read"], count(g))
                if st is CROSS:
                    pe.wait_ge(s["qlo_done"], n_queries)
                for hh, bank in enumerate((o_ps, m_ps)):
                    h = hp * PAIR + hh
                    for j in range(QT):
                        c = hh * SQ + j * P
                        ins = mm(bank[:, j * (D + 2):(j + 1) * (D + 2)], u_sb[0:st.drows, hp % 2, c:c + P], bm[0:st.drows, h, :],
                                 start=True, stop=True)
                ins.then_inc(s["out_ready"], 1)

            def weights_copied(n):
                pe.wait_ge(w_act, act_count(NWG * (n + 1) - 1))
                pe.wait_ge(w_dve, dve_count(NWG * (n + 1) - 1))

            def attention(st):
                s = S[st.name]

                def key_parts(kp, t):
                    if st is SELF:
                        c = slice(t * P, (t + 1) * P)
                        return zt_hi[:, kp, c], zt_lo[:, kp, c]
                    c = slice(t * P, t * P + st.krows[t])
                    return ct_hi[:, kp, c], ct_lo[0:DC, kp, c]

                def queries(pr):
                    kp = pr.bs % 2
                    if pr.hp < st.ahead:
                        pe.wait_ge(s["zlo_done"], pr.b + 1)
                    pe.wait_ge(s["qlo_done"], count(pr.g))
                    if st is CROSS:
                        pe.wait_ge(s["out_read"], count(pr.g - st.ahead - 1))
                    for hh in range(PAIR):
                        dst = q_bank[st][0:st.qrows, hh * SQ:(hh + 1) * SQ]
                        h = pr.hp * PAIR + hh
                        ah, al = a_hi[:, h, 0:st.qrows], a_lo[:, h, 0:st.qrows]
                        zh, zl = zt_hi[:, kp, :], zt_lo[:, kp, :]
                        ins = three(dst, ah, al, zh, zl)
                    ins.then_inc(s["q_ready"], 1)

                def maxima(pr, groups, mx=mx_banks[st]):
                    kp, k = pr.bs % 2, pr.hp % st.nq
                    for n in groups:
                        if n == 0:
                            pe.wait_ge(s["qhi_done"], pr.g + 1)
                            if st is CROSS:
                                pe.wait_ge(s["mx_read"], mx_count(st, Pair(pr.b, 0, 0, NP_)))
                        pe.wait_ge(s["mx_read"], count(mx_count(st, pr) + n + 1 - len(mx)))
                        if st is SELF:
                            for j in range(QT):
                                c = (QT * n + j) * P
                                ins = mm(mx[n % len(mx)][:, j * SQ:(j + 1) * SQ], q_hi[:, k, c:c + P], zt_hi[:, kp, :],
                                         start=True, stop=True)
                        else:
                            c, x0, xw = n // 4 * P, MX0[n % 4], MXW[n % 4]
                            ins = mm(mx[n % len(mx)][:, 0:xw], q_hi[0:DC, k, c:c + P], ct_hi[0:DC, kp, x0:x0 + xw],
                                     start=True, stop=True)
                        ins.then_inc(s["mx_ready"], 1)

                def scores(pr, t):
                    kp, k, kr = pr.bs % 2, pr.hp % st.nq, st.krows[t]
                    if t == 0:
                        pe.wait_ge(s["mrow_in"][k], (pr.g // st.nq + 1) * 64)
                        pe.wait_ge(s["qlo_done"], pr.g + 1)
                    d = st.back(pr.hp, t)
                    if d <= NSB:
                        pe.wait_ge(s["exp_done"], count(pr.g * st.nt + t - d + 1))
                    dst = s_ps[st.bank(pr.hp, t)][0:kr, :]
                    kh, kl = key_parts(kp, t)
                    r = st.drows
                    mm(dst, kh, q_hi[0:r, k, :], start=True, stop=False)
                    mm(dst, kh[0:st.qrows], q_lo[0:st.qrows, k, :], start=False, stop=False)
                    mm(dst, kl, q_hi[0:st.qrows, k, :], start=False, stop=True).then_inc(s["scores_ready"], 1)

                def values(pr, t):
                    kp, k, kr = pr.bs % 2, st.slot(pr.hp, t), st.krows[t]
                    if t == 0:
                        pe.wait_ge(s["u_copied"], count(pr.g))
                        if st is CROSS and pr.hp == 0:
                            pe.wait_ge(s["vlo_done"], 2 * pr.b + 2)
                    pe.wait_ge(s["plo_done"], pr.g * st.nt + t + 1)
                    if st is SELF:
                        vh, vl = zn_hi[:, kp, t, :], zn_lo[:, kp, t, :]
                    else:
                        vh, vl = cn_hi[0:kr, kp, t, 0:DC + 1], cn_lo[0:kr, kp, t, 0:DC + 1]
                    three(u_ps[0:st.drows, :], vh, vl, p_hi[0:kr, k, :], p_lo[0:kr, k, :],
                          t == 0, t == st.nt - 1).then_inc(s["pv_done"], 1)

                def body(pr, last):
                    steps, nxt = plan(st, pr, last)
                    for t in range(st.nt):
                        ahead = tile_ahead(st, pr, t, LEAD_PE, last)
                        if ahead:
                            scores(*ahead)
                        after = []
                        for what, arg in steps[t]:
                            if what == "z":
                                z_transposed(st, pr.b + 1, (pr.bs + 1) % 2, nxt.g + 1, pr.g)
                            if what == "prep":
                                context_groups(arg, pr.b + 1, (pr.bs + 1) % 2)
                            if what == "q":
                                queries(nxt)
                            if what == "mx":
                                maxima(*arg)
                            if what == "out" and not (isinstance(pr.g, int) and pr.g == 0):
                                args = (pr.g - 1, (pr.hp - 1) % NP_, nxt.g + 1 if nxt else B * NP_)
                                if st is SELF:
                                    after = [args]
                                else:
                                    outputs(st, *args)
                        values(pr, t)
                        for g, hp, n_queries in after:
                            outputs(st, g, hp, n_queries)

                pe.wait_ge(w_dve, dve_count(NWG * STAGES.index(st) + 9))
                for what, arg in start(st):
                    if what == "q":
                        queries(arg)
                    if what == "b":
                        b_product(STAGES.index(st), arg)
                    if what == "mx":
                        maxima(*arg, FIRST_MX[st])
                weights_copied(STAGES.index(st))
                for pr, t in first_tiles(st, LEAD_PE):
                    scores(pr, t)
                pairs(pe, st, body)

            def feed_forward():
                pe.wait_ge(ff_in, 32)
                pe.wait_ge(S["cross"]["exp_done"], B * NP_ * CT)
                for k in range(2):
                    mm(s_ps[k][:], mt[:, 3, :], raw[:, 0, k * 512:(k + 1) * 512],
                       start=True, stop=True).then_inc(wff_ready, 1)
                transposed(0)
                outputs(CROSS, B * NP_ - 1, NP_ - 1, B * NP_)
                transposed(1)
                pe.wait_ge(wff_lo, 2)
                first(0)
                first(1)
                transposed(2)
                second(0)
                first(2)
                transposed(3)
                second(1)
                first(3)
                second(2)
                second(3)

            def transposed(c):
                pe.wait_ge(FFN["z_made"], c + 1)
                if c >= 2:
                    pe.wait_ge(S["cross"]["out_read"], B * NP_)
                for i in range(4):
                    ins = nc.tensor.transpose(t_ps[c][:, i * P:(i + 1) * P], z[:, c % 2, i, :], ident[:])
                ins.then_inc(FFN["zt_ready"], 1)

            def first(c):
                pe.wait_ge(ffz_lo, c + 1)
                for f in range(FC):
                    pe.wait_ge(act_done, count(FC * c + f - 1))
                    for bank, col in ((gate_ps[f % 2], (FC + f) * P), (lin_ps[f % 2], f * P)):
                        three(bank[:], w1_hi[:, col:col + P], w1_lo[:, col:col + P], q_hi[:, c, :],
                              q_lo[:, c, :]).then_inc(ff1_ready, 1)

            def second(c):
                pe.wait_ge(act_done, FC * (c + 1))
                pe.wait_ge(ff_added, count(c - 1))
                for j in range(4):
                    for f in range(FC):
                        ins = mm(ff2_ps[c % 2][:, j * D:(j + 1) * D], ffx(c)[:, f * 512 + j * P:f * 512 + (j + 1) * P],
                                 w2[:, f, :], start=f == 0, stop=f == FC - 1)
                ins.then_inc(ff2_ready, 1)

            weights(0, {Z_AFTER: [lambda: z_transposed(SELF, 0, 0, 0, 0)]})
            attention(SELF)

            def z_first():
                pe.wait_ge(S["self"]["out_read"], B * NP_)
                z_transposed(CROSS, 0, 0, 0, 0)

            weights(1, {LAST_AFTER: [lambda: outputs(SELF, B * NP_ - 1, NP_ - 1, B * NP_)], Z_AFTER: [z_first]})
            attention(CROSS)
            feed_forward()


_NAMES = ("wq1", "wk1", "wv1", "wo1", "bo1", "g1", "b1", "wq2", "wk2", "wv2", "wo2", "bo2", "g2", "b2",
          "w_ff1", "b_ff1", "w_ff2", "b_ff2", "g3", "b3")


def kernel(**inputs):
    import numpy as np
    import concourse.bacc as bacc
    from concourse.bass_utils import run_bass_kernel_spmd

    nc = bacc.Bacc("TRN2", target_bir_lowering=False, num_devices=1)
    arrays, aps = {}, {}
    for name in ("x", "ctx_768") + tuple(f"L0_xattn_{n}" for n in _NAMES):
        a = np.ascontiguousarray(inputs[name])
        arrays[f"in_{name}"] = a
        aps[name] = nc.dram_tensor(f"in_{name}", a.shape, mybir.dt.from_np(a.dtype), kind="ExternalInput").ap()
    out = nc.dram_tensor("out", inputs["x"].shape, F32, kind="ExternalOutput").ap()
    build(nc, aps["x"], aps["ctx_768"], {n: aps[f"L0_xattn_{n}"] for n in _NAMES}, out)
    r = run_bass_kernel_spmd(nc, [arrays], core_ids=[0])
    return r.results[0]["out"]
```
